# Optimizing a Trainium2 kernel written in Bass

```python
import numpy as np
import jax
import jax.numpy as jnp

def _softmax(x, axis=-1):
    return jax.nn.softmax(x, axis=axis)

def _gelu(x):
    return jax.nn.gelu(x, approximate=True)

def _silu(x):
    return jax.nn.silu(x)

def _sigmoid(x):
    return jax.nn.sigmoid(x)

def _layernorm(x, axis=-1, eps=1e-05):
    m = jnp.mean(x, axis=axis, keepdims=True)
    v = jnp.var(x, axis=axis, keepdims=True)
    return (x - m) / jnp.sqrt(v + eps)

def _scatter_add(tgt, idx, src, axis=0):
    return tgt.at[idx].add(src)

def _segment_sum(src, seg, n):
    return jax.ops.segment_sum(src, seg, n)
kernel_name = 'mk_xattn_ffn_d1_seqx_r4_955910'

def setup_inputs(seed: int=0):
    np.random.seed(seed)
    _w = jnp.asarray

    def _rec_inputs():
        import jax
        import jax.numpy as jnp
        _rk = jax.random.key(seed)
        x = -0.000125 + 0.9999 * jax.random.normal(jax.random.fold_in(_rk, 1), (32, 256, 256), jnp.float32)
        _lenS = 256 - jax.random.randint(jax.random.fold_in(_rk, 7), (32,), 0, max(1, 256 // 4) + 1, jnp.int32)
        _lenS2 = 77 - jax.random.randint(jax.random.fold_in(_rk, 8), (32,), 0, max(1, 77 // 4) + 1, jnp.int32)
        _ctx_1024P = jax.random.normal(jax.random.fold_in(_rk, 11), (32, 16, 256), jnp.float32)
        _ctx_1024c = jax.random.dirichlet(jax.random.fold_in(_rk, 511), 0.3 * jnp.ones((16,), jnp.float32), (32, 77))
        _ctx_1024t = jnp.einsum('bsk,bkd->bsd', _ctx_1024c, _ctx_1024P)
        _ctx_1024t = _ctx_1024t * jax.lax.rsqrt(jnp.mean(jnp.square(_ctx_1024t)) + 1e-12) * 0.953939
        ctx_1024 = -1.39393e-06 + 0.999914 * (_ctx_1024t + 0.3 * jax.random.normal(jax.random.fold_in(_rk, 611), (32, 77, 256), jnp.float32))
        _validS = jnp.arange(256)[None, :] < _lenS[:, None]
        _validS2 = jnp.arange(77)[None, :] < _lenS2[:, None]
        _causal = jnp.tril(jnp.ones((256, 256), dtype=bool))
        mask_BxS2_bf0 = jnp.logical_not(jnp.ones((32, 77), dtype=bool))
        return (x, ctx_1024, mask_BxS2_bf0)
    x, ctx_1024, mask_BxS2_bf0 = _rec_inputs()

    def _L0_xattn_setup():
        import jax, jax.numpy as jnp
        import numpy as np
        B, LX, LY, D = (32, 256, 128, 256)
        key = jax.random.key(seed)
        k1, k2, k3, k4 = jax.random.split(key, 4)
        x = jax.random.normal(k1, (B, LX, D), dtype=jnp.float32)
        y = jax.random.normal(k2, (B, LY, D), dtype=jnp.float32)
        y_mask = jnp.zeros((B, LY), dtype=bool)
        W = jax.random.normal(k3, (D, D), dtype=jnp.float32) * (1.0 / np.sqrt(D))
        b = jax.random.normal(k4, (D,), dtype=jnp.float32) * 0.01
        return {'x': x, 'y': y, 'y_mask': y_mask, 'W': W, 'b': b}
    _L0_xattn_all = _L0_xattn_setup()
    _L0_xattn_in = {k: v for k, v in _L0_xattn_all.items() if k in ('W', 'b')}
    del _L0_xattn_all

    def _L0_ffn_setup():
        import jax, jax.numpy as jnp
        import numpy as np
        DIM = 256

        def _reference_tuple_inner(x, W_r, W_k, W_v, mu_r, mu_k):
            B, T, C = x.shape
            x_prev = jnp.concatenate([jnp.zeros((B, 1, C), x.dtype), x[:, :-1, :]], axis=1)
            xr = mu_r * x + (1.0 - mu_r) * x_prev
            xk = mu_k * x + (1.0 - mu_k) * x_prev
            r = jax.nn.sigmoid(jnp.einsum('btc,dc->btd', xr, W_r))
            k = jnp.einsum('btc,dc->btd', xk, W_k)
            k_act = jnp.square(jax.nn.relu(k))
            out = r * jnp.einsum('btc,dc->btd', k_act, W_v)
            new_state = x[:, -1, :]
            return (out, new_state)
        key = jax.random.key(seed)
        ks = jax.random.split(key, 6)
        B, T, C = (8, 512, DIM)
        x = jax.random.normal(ks[0], (B, T, C), dtype=jnp.float32)
        s = 1.0 / np.sqrt(C)
        W_r = jax.random.uniform(ks[1], (C, C), jnp.float32, -s, s)
        W_k = jax.random.uniform(ks[2], (C, C), jnp.float32, -s, s)
        W_v = jax.random.uniform(ks[3], (C, C), jnp.float32, -s, s)
        mu_r = jax.random.uniform(ks[4], (C,), jnp.float32)
        mu_k = jax.random.uniform(ks[5], (C,), jnp.float32)
        return {'x': x, 'W_r': W_r, 'W_k': W_k, 'W_v': W_v, 'mu_r': mu_r, 'mu_k': mu_k}
    _L0_ffn_all = _L0_ffn_setup()
    _L0_ffn_in = {k: v for k, v in _L0_ffn_all.items() if k in ('W_r', 'W_k', 'W_v', 'mu_r', 'mu_k')}
    del _L0_ffn_all
    return {'x': x, 'ctx_1024': ctx_1024, 'mask_BxS2_bf0': mask_BxS2_bf0, 'L0_xattn_W': _L0_xattn_in['W'], 'L0_xattn_b': _L0_xattn_in['b'], 'L0_ffn_W_r': _L0_ffn_in['W_r'], 'L0_ffn_W_k': _L0_ffn_in['W_k'], 'L0_ffn_W_v': _L0_ffn_in['W_v'], 'L0_ffn_mu_r': _L0_ffn_in['mu_r'], 'L0_ffn_mu_k': _L0_ffn_in['mu_k']}

def reference(x, ctx_1024, mask_BxS2_bf0, L0_xattn_W, L0_xattn_b, L0_ffn_W_r, L0_ffn_W_k, L0_ffn_W_v, L0_ffn_mu_r, L0_ffn_mu_k):
    import jax
    import jax.numpy as jnp

    def _L0_xattn_ref(x, y, y_mask, W, b):
        import jax, jax.numpy as jnp
        import numpy as np
        B, LX, LY, D = (32, 256, 128, 256)
        x_proj = jax.nn.relu(jnp.einsum('bxd,ed->bxe', x, W) + b)
        y_proj = jax.nn.relu(jnp.einsum('byd,ed->bye', y, W) + b)
        scores = jnp.einsum('bxd,byd->bxy', x_proj, y_proj)
        scores = jnp.where(y_mask[:, None, :], -jnp.inf, scores)
        att = jax.nn.softmax(scores, axis=-1)
        return jnp.einsum('bxy,byd->bxd', att, y)

    def _L0_ffn_ref(x, W_r, W_k, W_v, mu_r, mu_k):
        import jax, jax.numpy as jnp
        import numpy as np
        DIM = 256

        def _reference_tuple_inner(x, W_r, W_k, W_v, mu_r, mu_k):
            B, T, C = x.shape
            x_prev = jnp.concatenate([jnp.zeros((B, 1, C), x.dtype), x[:, :-1, :]], axis=1)
            xr = mu_r * x + (1.0 - mu_r) * x_prev
            xk = mu_k * x + (1.0 - mu_k) * x_prev
            r = jax.nn.sigmoid(jnp.einsum('btc,dc->btd', xr, W_r))
            k = jnp.einsum('btc,dc->btd', xk, W_k)
            k_act = jnp.square(jax.nn.relu(k))
            out = r * jnp.einsum('btc,dc->btd', k_act, W_v)
            new_state = x[:, -1, :]
            return (out, new_state)
        return _reference_tuple_inner(x, W_r, W_k, W_v, mu_r, mu_k)[0]
    x = x + _L0_xattn_ref(_layernorm(x, axis=-1), ctx_1024, mask_BxS2_bf0, L0_xattn_W, L0_xattn_b)
    x = x + _L0_ffn_ref(_layernorm(x, axis=-1), L0_ffn_W_r, L0_ffn_W_k, L0_ffn_W_v, L0_ffn_mu_r, L0_ffn_mu_k)
    return x

_drawn_inputs = setup_inputs


def setup_inputs(seed=0):
    import zlib

    import numpy as np

    out = dict(_drawn_inputs(seed))
    spreads = {}
    factors = {'L0_xattn_b': 3.457, 'L0_ffn_W_r': 4.042, 'L0_ffn_mu_r': 8.0}
    for name, (base, spread) in spreads.items():
        noise = np.random.default_rng([zlib.crc32(name.encode()), seed]).standard_normal(out[name].shape)
        drawn = base * np.exp(spread * noise) if base else spread * noise
        out[name] = jnp.asarray(drawn.astype(out[name].dtype))
    for name, factor in factors.items():
        out[name] = (out[name] * factor).astype(out[name].dtype)
    return out
```

```python
import concourse.bass as bass
from concourse import mybir
from contextlib import ExitStack


def xattn_rwkv_ffn_kernel(nc, x, ctx, mask, W, b, W_r, W_k, W_v, mu_r, mu_k, out):
    f32, f32r, u8 = mybir.dt.float32, mybir.dt.float32r, mybir.dt.uint8
    ALU, ACT, AX = mybir.AluOpType, mybir.ActivationFunctionType, mybir.AxisListType

    B, L, D = x.shape
    K = ctx.shape[1]
    P = 128
    PAIRS = B // 2
    T = 2 * L // P
    TB = L // P
    N = 2 * L
    C = D // P
    KP = 2 * K
    EPS = 1e-5
    FIRST, LAST = -1, PAIRS + 1
    LOOP = (4, PAIRS - 2)

    x_rows = x.rearrange("b (t p) d -> p (b t) d", p=P)
    out_rows = out.rearrange("b (t p) d -> p (b t) d", p=P)
    ctx_rows = ctx.rearrange("b k d -> k b d")

    es = ExitStack()
    with es:
        def sb(name, shape, dt=f32):
            return es.enter_context(nc.sbuf_tensor(name, shape, dt))

        def sem(name):
            return es.enter_context(nc.semaphore(name))

        def ring(name, shape, dt=f32):
            return [sb(f"{name}{i}", shape, dt) for i in range(2)]

        ident = sb("ident", [P, P])
        wT_hi = sb("wT_hi", [P, 4, C, D], f32r)
        wT_lo = sb("wT_lo", [P, 4, C, D], f32r)
        XP, WR, WK, WV = range(4)
        bias_col = sb("bias_col", [P, C])
        mu = sb("mu", [P, 2, C])
        one_minus_mu = sb("one_minus_mu", [P, 2, C])
        neg_half = sb("neg_half", [P, T])
        mask_u8 = sb("mask_u8", [P, B * K], u8)
        mask_bias = sb("mask_bias", [P, B, K])
        X = sb("X", [P, B * TB, D])
        xn = sb("xn", [P, T, D])
        bn1 = sb("bn1", [P, T, 6])
        mv1 = sb("mv1", [P, T, 2])
        ve1 = sb("ve1", [P, T])
        rstd1 = sb("rstd1", [P, T])
        xnT_hi = sb("xnT_hi", [P, C, N], f32r)
        xnT_lo = sb("xnT_lo", [P, C, N], f32r)
        y = ring("y", [K, 2, D])
        yT_hi = sb("yT_hi", [P, C, KP], f32r)
        yT_lo = sb("yT_lo", [P, C, KP], f32r)
        xp = sb("xp", [P, C, N])
        yp = sb("yp", [P, C, KP])
        sc = sb("sc", [P, T, K])
        sc0 = sb("sc0", [P, T, K])
        mx = sb("mx", [P, T])
        prob = sb("prob", [P, T, K])
        psums = sb("psums", [P, T])
        rinv = sb("rinv", [P, T])
        probT = sb("probT", [K, N])
        x1_both = sb("x1", [P, 2, T, D])
        x1 = [x1_both[:, i, :, :] for i in range(2)]
        w_rows = x1_both[:, :, :, :].rearrange("p i (m c) d -> p (i m) c d", c=C)
        bn2 = sb("bn2", [P, T, 6])
        mv2 = sb("mv2", [P, T, 2])
        ve2 = sb("ve2", [P, T])
        rstd2 = sb("rstd2", [P, T])
        nm2 = sb("nm2", [P, T])
        xn2 = sb("xn2", [P, T, D])
        z = sb("z", [P, C, 2, L + 1])
        mu_z = sb("mu_z", [P, 2, C, N])
        mix = sb("mix", [P, 2, C, N])
        mix_hi = ring("mix_hi", [P, 2, C, N], f32r)
        mix_lo = ring("mix_lo", [P, 2, C, N], f32r)
        kact = sb("kact", [P, C, N])
        kact_hi = sb("kact_hi", [P, C, N], f32r)
        kact_lo = sb("kact_lo", [P, C, N], f32r)
        th = sb("th", [P, T, D])
        g = sb("g", [P, T, D])

        swap = [es.enter_context(nc.psum_tensor(f"swap{i}", [P, 2, 512], f32)) for i in range(2)]
        fixed = es.enter_context(nc.psum_tensor("fixed", [P, 2, 512], f32))
        key_bank = es.enter_context(nc.psum_tensor("key_bank", [P, 512], f32))
        score_bank = es.enter_context(nc.psum_tensor("score_bank", [P, 512], f32))

        def rows(bank2):
            return bank2[:, :, :].rearrange("p c (t d) -> p (c t) d", d=D)

        w_loaded, small_loaded = sem("w_loaded"), sem("small_loaded")
        x_loaded = [sem("x_loaded0"), sem("x_loaded1")]
        y_loaded = [sem("y_loaded0"), sem("y_loaded1")]
        stored = sem("stored")
        ident_ready, pool_const = sem("ident_ready"), sem("pool_const")
        wT_done, wT_hi_ready, wT_lo_ready = sem("wT_done"), sem("wT_hi_ready"), sem("wT_lo_ready")
        dve_const = sem("dve_const")
        xnT_done, yT_done = sem("xnT_done"), sem("yT_done")
        xp_done, yp_done = sem("xp_done"), sem("yp_done")
        score_done, probT_done, attn_done = sem("score_done"), sem("probT_done"), sem("attn_done")
        zT_done, k_done, r_done, kv_done = sem("zT_done"), sem("k_done"), sem("r_done"), sem("kv_done")
        xnT_hi_ready, yT_hi_ready = sem("xnT_hi_ready"), sem("yT_hi_ready")
        xp_ready, yp_ready = sem("xp_ready"), sem("yp_ready")
        krelu_ready, kact_ready, kact_hi_ready = sem("krelu_ready"), sem("kact_ready"), sem("kact_hi_ready")
        z_ready, mu_z_ready = sem("z_ready"), sem("mu_z_ready")
        prob_ready, th_ready, probT_ready = sem("prob_ready"), sem("th_ready"), sem("probT_ready")
        x1_ready, bn2_ready, mv2_ready = sem("x1_ready"), sem("bn2_ready"), sem("mv2_ready")
        bn1_ready, mv1_ready, xn_ready = sem("bn1_ready"), sem("mv1_ready"), sem("xn_ready")
        sc_ready, mx_ready, sc0_ready = sem("sc_ready"), sem("mx_ready"), sem("sc0_ready")
        psums_ready, rinv_ready = sem("psums_ready"), sem("rinv_ready")
        mix_ready, mix_hi_ready, mix_lo_ready = sem("mix_ready"), sem("mix_hi_ready"), sem("mix_lo_ready")
        g_ready = sem("g_ready")
        xnT_lo_ready, yT_lo_ready = sem("xnT_lo_ready"), sem("yT_lo_ready")
        ve1_ready, rstd1_ready = sem("ve1_ready"), sem("rstd1_ready")
        ve2_ready, rstd2_ready, xn2_ready = sem("ve2_ready"), sem("rstd2_ready"), sem("xn2_ready")
        kact_lo_ready, mixk_lo_ready, res_ready = sem("kact_lo_ready"), sem("mixk_lo_ready"), sem("res_ready")

        def live(p):
            return not isinstance(p, int) or 0 <= p < PAIRS

        def some(p):
            return not isinstance(p, int) or p >= 0

        def steps(eng, step):
            for u in range(FIRST, LOOP[0]):
                step(u, u % 2)
            with eng.Fori(LOOP[0] // 2, LOOP[1] // 2) as i:
                for s in range(2):
                    step(2 * i + s, s)
            for u in range(LOOP[1], LAST + 1):
                step(u, u % 2)

        block = es.enter_context(nc.Block())

        @block.sync
        def _(sp):
            def load_x(p, par):
                if some(p - 2):
                    sp.wait_ge(x_loaded[par], 8 * (p - par))
                sp.dma_start(X[:, bass.ds(T * p, T), :], x_rows[:, bass.ds(T * p, T), :]).then_inc(x_loaded[par], 16)

            def load_y(p, par):
                if some(p - 2):
                    sp.wait_ge(attn_done, 2 * (p - 2) + 2)
                sp.dma_start(y[par][:, :, :], ctx_rows[:, bass.ds(2 * p, 2), :]).then_inc(y_loaded[par], 16)

            load_x(0, 0)
            for m, w in enumerate((W, W_r, W_k, W_v)):
                sp.dma_start(w_rows[:, m, :, :], w.rearrange("(c p) d -> p c d", p=P)).then_inc(w_loaded, 16)

            def step(u, s):
                if live(u + 2):
                    load_x(u + 2, s)
                if live(u + 1):
                    load_y(u + 1, 1 - s)
                if live(u - 2):
                    sp.wait_ge(res_ready, (u - 2) + 1)
                    sp.dma_start(out_rows[:, bass.ds(T * (u - 2), T), :], g[:, :, :]).then_inc(stored, 16)

            steps(sp, step)
            sp.wait_ge(stored, 16 * PAIRS)

        @block.gpsimd
        def _(pool):
            pool.memset(ident[:, :], 0.0).then_inc(ident_ready, 1)
            pool.memset(neg_half[:, :], -0.5).then_inc(pool_const, 1)
            pool.wait_ge(ident_ready, 1)
            pool.affine_select(out=ident[:, :], in_=ident[:, :], compare_op=ALU.not_equal, fill=1.0,
                               base=0, pattern=[[-1, P]], channel_multiplier=1).then_inc(ident_ready, 1)
            pool.memset(z[:, :, :, 0:1], 0.0).then_inc(pool_const, 1)
            pool.wait_ge(pool_const, 2)

            def step(u, s):
                p = u + 1
                if live(p):
                    pool.wait_ge(mv1_ready, p + 1)
                    pool.nop(nofuse=True)
                    pool.tensor_scalar(ve1[:, :], mv1[:, :, 1], EPS, None, ALU.add).then_inc(ve1_ready, 1)
                    pool.wait_ge(ve1_ready, p + 1)
                    pool.tensor_tensor(rstd1[:, :], ve1[:, :], neg_half[:, :], ALU.pow).then_inc(rstd1_ready, 1)
                p = u - 1
                if live(p):
                    pool.wait_ge(mv2_ready, p + 1)
                    pool.nop(nofuse=True)
                    pool.tensor_scalar(ve2[:, :], mv2[:, :, 1], EPS, None, ALU.add).then_inc(ve2_ready, 1)
                    pool.tensor_scalar(nm2[:, :], mv2[:, :, 0], -1.0, None, ALU.mult).then_inc(rstd2_ready, 1)
                    pool.wait_ge(ve2_ready, p + 1)
                    pool.tensor_tensor(rstd2[:, :], ve2[:, :], neg_half[:, :], ALU.pow).then_inc(rstd2_ready, 1)
                    pool.wait_ge(rstd2_ready, 2 * p + 2)
                    if some(p - 1):
                        pool.wait_ge(zT_done, 2 * p)
                    pool.nop(nofuse=True)
                    for t in range(T):
                        i = pool.tensor_scalar(xn2[:, t, :], x1[1 - s][:, t, :], nm2[:, t:t + 1],
                                               rstd2[:, t:t + 1], ALU.add, ALU.mult)
                    i.then_inc(xn2_ready, 1)
                p = u - 2
                if live(p):
                    pool.wait_ge(kact_hi_ready, p + 1)
                    if some(p - 1):
                        pool.wait_ge(kv_done, 2 * p)
                    pool.tensor_tensor(kact_lo[:, :, :], kact[:, :, :], kact_hi[:, :, :].bitcast(f32),
                                       ALU.subtract).then_inc(kact_lo_ready, 1)
                p = u - 1
                if live(p):
                    pool.wait_ge(mix_hi_ready, 2 * p + 1)
                    if some(p - 2):
                        pool.wait_ge(k_done, 2 * (p - 1))
                    pool.tensor_tensor(mix_lo[1 - s][:, 1, :, :], mix[:, 1, :, :],
                                       mix_hi[1 - s][:, 1, :, :].bitcast(f32), ALU.subtract).then_inc(mixk_lo_ready, 1)
                p = u - 2
                if live(p):
                    pool.wait_ge(g_ready, 2 * p + 2)
                    pool.tensor_tensor(g[:, :, :], g[:, :, :], x1[s][:, :, :], ALU.add).then_inc(res_ready, 1)

            steps(pool, step)

        @block.scalar
        def _(act):
            with nc.allow_non_contiguous_dma(reason="three vectors of one value a partition"):
                act.dma_start(bias_col[:, :], b.rearrange("(c p) -> p c", p=P)).then_inc(small_loaded, 16)
                for i, m in enumerate((mu_r, mu_k)):
                    act.dma_start(mu[:, i, :], m.rearrange("(c p) -> p c", p=P)).then_inc(small_loaded, 16)
            act.dma_start(mask_u8[:, :], mask.rearrange("b k -> (b k)").partition_broadcast(P)).then_inc(small_loaded, 16)
            act.wait_ge(small_loaded, 64)
            for m in range(4):
                act.wait_ge(wT_done, m + 1)
                bank = (swap[0], swap[1])[m // 2][:, m % 2, :]
                act.activation(wT_hi[:, m, :, :], bank, ACT.Copy,
                               scale=0.5 if m == WV else 1.0).then_inc(wT_hi_ready, 1)

            def step(u, s):
                p = u
                if live(p):
                    if some(p - 1):
                        act.wait_ge(score_done, p)
                    for c in range(C):
                        act.wait_ge(xp_done, C * p + c + 1)
                        act.activation(xp[:, c, :], swap[s][:, c, :], ACT.Relu,
                                       bias=bias_col[:, c:c + 1]).then_inc(xp_ready, 1)
                    act.wait_ge(yp_done, p + 1)
                    for c in range(C):
                        act.activation(yp[:, c, :], key_bank[:, c * KP:(c + 1) * KP], ACT.Relu,
                                       bias=bias_col[:, c:c + 1]).then_inc(yp_ready, 1)
                p = u - 2
                if live(p):
                    if some(p - 1):
                        act.wait_ge(kact_lo_ready, p)
                    for c in range(C):
                        act.wait_ge(k_done, C * p + c + 1)
                        act.activation(kact[:, c, :], swap[1 - s][:, c, :], ACT.Relu).then_inc(krelu_ready, 1)
                    act.wait_ge(krelu_ready, C * p + C)
                    act.activation(kact[:, :, :], kact[:, :, :], ACT.Square).then_inc(kact_ready, 1)
                    act.wait_ge(kact_ready, p + 1)
                    if some(p - 1):
                        act.wait_ge(kv_done, 2 * p)
                    act.activation(kact_hi[:, :, :], kact[:, :, :], ACT.Copy).then_inc(kact_hi_ready, 1)
                p = u - 1
                if live(p):
                    if some(p - 1):
                        act.wait_ge(mix_ready, 2 * C * p)
                    for c in range(C):
                        act.wait_ge(zT_done, C * p + c + 1)
                        act.activation(z[:, c, :, 1:L + 1], swap[s][:, c, :].rearrange("p (b l) -> p b l", b=2),
                                       ACT.Copy).then_inc(z_ready, 1)
                        for m in (1, 0):
                            act.activation(mu_z[:, m, c, :], swap[s][:, c, :], ACT.Copy,
                                           scale=mu[:, m, c:c + 1]).then_inc(mu_z_ready, 1)
                p = u
                if live(p):
                    act.wait_ge(sc0_ready, p + 1)
                    if some(p - 1):
                        act.wait_ge(probT_done, p)
                    act.activation(prob[:, :, :], sc0[:, :, :], ACT.Exp).then_inc(prob_ready, 1)
                p = u - 2
                if live(p):
                    if some(p - 1):
                        act.wait_ge(g_ready, 2 * p)
                    for h in range(2):
                        act.wait_ge(r_done, 2 * p + h + 1)
                        act.activation(th[:, 2 * h:2 * h + 2, :], rows(fixed)[:, 2 * h:2 * h + 2, :], ACT.Tanh,
                                       scale=0.5).then_inc(th_ready, 1)
                p = u
                if live(p):
                    act.wait_ge(probT_done, p + 1)
                    if some(p - 1):
                        act.wait_ge(attn_done, 2 * p)
                    act.activation(probT[:, :], key_bank[0:K, 0:N], ACT.Copy).then_inc(probT_ready, 1)
                p = u + 1
                if live(p):
                    if some(p - 1):
                        act.wait_ge(yp_done, p)
                    for c in range(C):
                        act.wait_ge(xnT_done, C * p + c + 1)
                        act.activation(xnT_hi[:, c, :], fixed[:, c, :], ACT.Copy).then_inc(xnT_hi_ready, 1)
                    act.wait_ge(yT_done, p + 1)
                    act.activation(yT_hi[:, :, :], score_bank[:, 0:C * KP].rearrange("p (c k) -> p c k", c=C),
                                   ACT.Copy).then_inc(yT_hi_ready, 1)

            steps(act, step)

        @block.vector
        def _(dve):
            dve.wait_ge(small_loaded, 64)
            dve.tensor_scalar(one_minus_mu[:, :, :], mu[:, :, :], -1.0, 1.0, ALU.mult, ALU.add).then_inc(dve_const, 1)
            dve.tensor_scalar(mask_bias[:, :, :], mask_u8[:, :].rearrange("p (b k) -> p b k", k=K), -3e38, 3e38,
                              ALU.mult, ALU.mult).then_inc(dve_const, 1)
            for m in range(4):
                dve.wait_ge(wT_hi_ready, m + 1)
                bank = (swap[0], swap[1])[m // 2][:, m % 2, :].rearrange("p (c d) -> p c d", c=C)
                dve.scalar_tensor_tensor(wT_lo[:, m, :, :], bank, 0.5 if m == WV else 1.0,
                                         wT_hi[:, m, :, :].bitcast(f32), ALU.mult, ALU.subtract).then_inc(wT_lo_ready, 1)
            dve.wait_ge(dve_const, 2)
            dve.wait_ge(pool_const, 2)

            def step(u, s):
                p = u - 1
                if live(p):
                    dve.wait_ge(rinv_ready, p + 1)
                    if some(p - 2):
                        dve.wait_ge(res_ready, p - 1)
                    for t in range(T):
                        if t % TB == 0:
                            dve.wait_ge(attn_done, 2 * p + t // TB + 1)
                        dve.scalar_tensor_tensor(x1[1 - s][:, t, :], rows(swap[1 - s])[:, t, :], rinv[:, t:t + 1],
                                                 X[:, T * p + t, :], ALU.mult, ALU.add).then_inc(x1_ready, 1)
                    for t in range(T):
                        dve.wait_ge(x1_ready, T * p + t + 1)
                        dve.bn_stats(bn2[:, t, :], x1[1 - s][:, t, :]).then_inc(bn2_ready, 1)
                    if some(p - 1):
                        dve.wait_ge(rstd2_ready, 2 * p)
                    for t in range(T):
                        dve.wait_ge(bn2_ready, T * p + t + 1)
                        dve.nop(nofuse=True)
                        i = dve.bn_aggr(mv2[:, t, :], bn2[:, t, :])
                    i.then_inc(mv2_ready, 1)
                p = u + 1
                if live(p):
                    dve.wait_ge(x_loaded[1 - s], 8 * (p - (1 - s)) + 16)
                    for t in range(T):
                        dve.bn_stats(bn1[:, t, :], X[:, T * p + t, :]).then_inc(bn1_ready, 1)
                    if some(p - 1):
                        dve.wait_ge(rstd1_ready, p)
                    for t in range(T):
                        dve.wait_ge(bn1_ready, T * p + t + 1)
                        dve.nop(nofuse=True)
                        i = dve.bn_aggr(mv1[:, t, :], bn1[:, t, :])
                    i.then_inc(mv1_ready, 1)
                p = u
                if live(p):
                    dve.wait_ge(score_done, p + 1)
                    dve.tensor_tensor(sc[:, :, :].rearrange("p (b t) k -> p b t k", b=2),
                                      score_bank[:, 0:T * K].rearrange("p (b t k) -> p b t k", b=2, k=K),
                                      mask_bias[:, bass.ds(2 * p, 2), :].unsqueeze(2).to_broadcast([P, 2, TB, K]),
                                      ALU.add).then_inc(sc_ready, 1)
                    dve.wait_ge(sc_ready, p + 1)
                    dve.tensor_reduce(mx[:, :], sc[:, :, :], AX.X, ALU.max).then_inc(mx_ready, 1)
                    dve.wait_ge(mx_ready, p + 1)
                    dve.tensor_tensor(sc0[:, :, :], sc[:, :, :], mx[:, :].unsqueeze(2).to_broadcast([P, T, K]),
                                      ALU.subtract).then_inc(sc0_ready, 1)
                p = u + 1
                if live(p):
                    dve.wait_ge(rstd1_ready, p + 1)
                    if some(p - 1):
                        dve.wait_ge(xnT_done, C * p)
                    for t in range(T):
                        i = dve.tensor_scalar(xn[:, t, :], X[:, T * p + t, :], mv1[:, t, 0:1], rstd1[:, t:t + 1],
                                              ALU.subtract, ALU.mult)
                    i.then_inc(xn_ready, 1)
                p = u
                if live(p):
                    dve.wait_ge(prob_ready, p + 1)
                    dve.tensor_reduce(psums[:, :], prob[:, :, :], AX.X, ALU.add).then_inc(psums_ready, 1)
                    dve.wait_ge(psums_ready, p + 1)
                    dve.reciprocal(rinv[:, :], psums[:, :]).then_inc(rinv_ready, 1)
                p = u - 1
                if live(p):
                    if some(p - 1):
                        dve.wait_ge(mixk_lo_ready, p)
                    n = 0
                    for m in (1, 0):
                        for c in range(C):
                            dve.wait_ge(mu_z_ready, 2 * C * p + 2 * C if m == 0 else 2 * C * p + 2 * c + 1)
                            dve.scalar_tensor_tensor(mix[:, m, c, :].rearrange("p (b l) -> p b l", b=2),
                                                     z[:, c, :, 0:L], one_minus_mu[:, m, c:c + 1],
                                                     mu_z[:, m, c, :].rearrange("p (b l) -> p b l", b=2),
                                                     ALU.mult, ALU.add).then_inc(mix_ready, 1)
                        if m == 1:
                            if some(p - 2):
                                dve.wait_ge(r_done, 2 * (p - 1))
                            dve.wait_ge(mix_ready, 2 * C * p + C)
                            dve.tensor_copy(mix_hi[1 - s][:, 1, :, :], mix[:, 1, :, :]).then_inc(mix_hi_ready, 1)
                    dve.wait_ge(mix_ready, 2 * C * p + 2 * C)
                    dve.tensor_copy(mix_hi[1 - s][:, 0, :, :], mix[:, 0, :, :]).then_inc(mix_hi_ready, 1)
                    dve.wait_ge(mix_hi_ready, 2 * p + 2)
                    dve.tensor_tensor(mix_lo[1 - s][:, 0, :, :], mix[:, 0, :, :],
                                      mix_hi[1 - s][:, 0, :, :].bitcast(f32), ALU.subtract).then_inc(mix_lo_ready, 1)
                p = u - 2
                if live(p):
                    if some(p - 1):
                        dve.wait_ge(stored, 16 * p)
                    for h in range(2):
                        dve.wait_ge(th_ready, 2 * p + h + 1)
                        dve.wait_ge(kv_done, 2 * p + h + 1)
                        dve.scalar_tensor_tensor(g[:, 2 * h:2 * h + 2, :], th[:, 2 * h:2 * h + 2, :], 1.0,
                                                 rows(swap[1 - s])[:, 2 * h:2 * h + 2, :], ALU.add,
                                                 ALU.mult).then_inc(g_ready, 1)
                p = u + 1
                if live(p):
                    for c in range(C):
                        dve.wait_ge(xnT_hi_ready, C * p + c + 1)
                        dve.tensor_tensor(xnT_lo[:, c, :], fixed[:, c, :], xnT_hi[:, c, :].bitcast(f32),
                                          ALU.subtract).then_inc(xnT_lo_ready, 1)
                    dve.wait_ge(yT_hi_ready, p + 1)
                    dve.tensor_tensor(yT_lo[:, :, :], score_bank[:, 0:C * KP].rearrange("p (c k) -> p c k", c=C),
                                      yT_hi[:, :, :].bitcast(f32), ALU.subtract).then_inc(yT_lo_ready, 1)

            steps(dve, step)

        @block.tensor
        def _(pe):
            pe.wait_ge(ident_ready, 2)
            pe.wait_ge(w_loaded, 64)
            for m in range(4):
                for ci in range(C):
                    for co in range(C):
                        i = pe.transpose(swap[m // 2][:, m % 2, ci * D + co * P:ci * D + (co + 1) * P],
                                         w_rows[:, m, co, ci * P:(ci + 1) * P], ident[:, :])
                i.then_inc(wT_done, 1)

            def three(o, st_hi, st_lo, mv_hi, mv_lo):
                for c in range(C):
                    pe.matmul(o, st_hi(c), mv_hi(c), start=(c == 0), stop=False)
                    pe.matmul(o, st_hi(c), mv_lo(c), start=False, stop=False)
                    i = pe.matmul(o, st_lo(c), mv_hi(c), start=False, stop=(c == C - 1))
                return i

            def step(u, s):
                p = u
                if live(p):
                    if isinstance(p, int) and p == 0:
                        pe.wait_ge(wT_lo_ready, 4)
                    if some(p - 3):
                        pe.wait_ge(g_ready, 2 * (p - 3) + 2)
                    pe.wait_ge(xnT_lo_ready, C * p + C)
                    for e in range(C):
                        three(swap[s][:, e, :], lambda c: wT_hi[:, XP, c, e * P:(e + 1) * P],
                              lambda c: wT_lo[:, XP, c, e * P:(e + 1) * P],
                              lambda c: xnT_hi[:, c, :], lambda c: xnT_lo[:, c, :]).then_inc(xp_done, 1)
                    pe.wait_ge(yT_lo_ready, p + 1)
                    for e in range(C):
                        i = three(key_bank[:, e * KP:(e + 1) * KP], lambda c: wT_hi[:, XP, c, e * P:(e + 1) * P],
                                  lambda c: wT_lo[:, XP, c, e * P:(e + 1) * P],
                                  lambda c: yT_hi[:, c, :], lambda c: yT_lo[:, c, :])
                    i.then_inc(yp_done, 1)
                p = u - 2
                if live(p):
                    pe.wait_ge(mixk_lo_ready, p + 1)
                    if live(u - 1):
                        pe.wait_ge(x1_ready, T * (u - 1) + T)
                    else:
                        pe.wait_ge(mu_z_ready, 2 * C * p + 2 * C)
                    for e in range(C):
                        three(swap[1 - s][:, e, :], lambda c: wT_hi[:, WK, c, e * P:(e + 1) * P],
                              lambda c: wT_lo[:, WK, c, e * P:(e + 1) * P],
                              lambda c: mix_hi[s][:, 1, c, :], lambda c: mix_lo[s][:, 1, c, :]).then_inc(k_done, 1)
                p = u
                if live(p):
                    pe.wait_ge(xp_ready, C * p + C)
                    pe.wait_ge(yp_ready, C * p + C)
                    for t in range(T):
                        bk = t // TB
                        for c in range(C):
                            i = pe.matmul(score_bank[:, t * K:(t + 1) * K], xp[:, c, t * P:(t + 1) * P],
                                          yp[:, c, bk * K:(bk + 1) * K], start=(c == 0), stop=(c == C - 1))
                    i.then_inc(score_done, 1)
                p = u - 1
                if live(p):
                    pe.wait_ge(xn2_ready, p + 1)
                    if not live(u):
                        pe.wait_ge(g_ready, 2 * (u - 3) + 2)
                    for c in range(C):
                        for t in range(T):
                            i = pe.transpose(swap[s][:, c, t * P:(t + 1) * P], xn2[:, t, c * P:(c + 1) * P],
                                             ident[:, :])
                        i.then_inc(zT_done, 1)
                p = u - 2
                if live(p):
                    pe.wait_ge(mix_lo_ready, p + 1)
                    if not live(u):
                        pe.wait_ge(th_ready, 2 * (u - 3) + 2)
                    for t in range(T):
                        i = three(rows(fixed)[:, t, :], lambda c: mix_hi[s][:, 0, c, t * P:(t + 1) * P],
                                  lambda c: mix_lo[s][:, 0, c, t * P:(t + 1) * P],
                                  lambda c: wT_hi[:, WR, c, :], lambda c: wT_lo[:, WR, c, :])
                        if t % 2:
                            i.then_inc(r_done, 1)
                p = u
                if live(p):
                    pe.wait_ge(prob_ready, p + 1)
                    for t in range(T):
                        i = pe.transpose(key_bank[0:K, t * P:(t + 1) * P], prob[:, t, :], ident[:, :])
                    i.then_inc(probT_done, 1)
                p = u - 2
                if live(p):
                    pe.wait_ge(kact_lo_ready, p + 1)
                    for t in range(T):
                        i = three(rows(swap[1 - s])[:, t, :], lambda c: kact_hi[:, c, t * P:(t + 1) * P],
                                  lambda c: kact_lo[:, c, t * P:(t + 1) * P],
                                  lambda c: wT_hi[:, WV, c, :], lambda c: wT_lo[:, WV, c, :])
                        if t % 2:
                            i.then_inc(kv_done, 1)
                p = u + 1
                if live(p):
                    pe.wait_ge(xn_ready, p + 1)
                    if some(u - 2):
                        pe.wait_ge(th_ready, 2 * (u - 2) + 2)
                    for c in range(C):
                        for t in range(T):
                            i = pe.transpose(fixed[:, c, t * P:(t + 1) * P], xn[:, t, c * P:(c + 1) * P], ident[:, :])
                        i.then_inc(xnT_done, 1)
                    pe.wait_ge(y_loaded[1 - s], 8 * (p - (1 - s)) + 16)
                    if some(p - 1):
                        pe.wait_ge(sc_ready, p)
                    for c in range(C):
                        for bk in range(2):
                            i = pe.transpose(score_bank[:, c * KP + bk * K:c * KP + (bk + 1) * K],
                                             y[1 - s][:, bk, c * P:(c + 1) * P], ident[0:K, 0:K])
                    i.then_inc(yT_done, 1)
                p = u
                if live(p):
                    pe.wait_ge(probT_ready, p + 1)
                    if some(p - 1):
                        pe.wait_ge(mu_z_ready, 2 * C * (p - 1) + 2 * C)
                    for t in range(T):
                        i = pe.matmul(rows(swap[s])[:, t, :], probT[:, t * P:(t + 1) * P],
                                      y[s][:, t // TB, :], start=True, stop=True)
                        if t % TB == TB - 1:
                            i.then_inc(attn_done, 1)

            steps(pe, step)


_INS = ['x', 'ctx_1024', 'mask_BxS2_bf0', 'L0_xattn_W', 'L0_xattn_b', 'L0_ffn_W_r', 'L0_ffn_W_k', 'L0_ffn_W_v',
        'L0_ffn_mu_r', 'L0_ffn_mu_k']


def kernel(**inputs):
    import numpy as _np
    import concourse.bacc as _bacc
    from concourse import mybir as _mybir
    from concourse.bass_utils import run_bass_kernel_spmd as _run

    nc = _bacc.Bacc("TRN2", target_bir_lowering=False, num_devices=1)
    arrays, args = {}, []
    for name in _INS:
        a = _np.ascontiguousarray(inputs[name])
        arrays[f"in_{name}_dram"] = a
        args.append(nc.dram_tensor(f"in_{name}_dram", a.shape, _mybir.dt.from_np(a.dtype), kind="ExternalInput").ap())
    shape = tuple(inputs["x"].shape)
    args.append(nc.dram_tensor("out_0_dram", shape, _mybir.dt.float32, kind="ExternalOutput").ap())
    xattn_rwkv_ffn_kernel(nc, *args)
    r = _run(nc, [arrays], core_ids=[0])
    return r.results[0]["out_0_dram"]
```

```python
import concourse.bass as bass
from concourse import mybir
from contextlib import ExitStack


def xattn_rwkv_ffn_kernel(nc, x, ctx, mask, W, b, W_r, W_k, W_v, mu_r, mu_k, out):
    f32, f32r, u8 = mybir.dt.float32, mybir.dt.float32r, mybir.dt.uint8
    ALU, ACT, AX = mybir.AluOpType, mybir.ActivationFunctionType, mybir.AxisListType

    B, L, D = x.shape
    K = ctx.shape[1]
    P = 128
    PAIRS = B // 2
    T = 2 * L // P
    TB = L // P
    N = 2 * L
    C = D // P
    KP = 2 * K
    EPS = 1e-5
    FIRST, LAST = -2, PAIRS + 1
    LOOP = (4, PAIRS - 2)

    x_rows = x.rearrange("b (t p) d -> p (b t) d", p=P)
    out_rows = out.rearrange("b (t p) d -> p (b t) d", p=P)
    ctx_rows = ctx.rearrange("b k d -> k b d")

    es = ExitStack()
    with es:
        def sb(name, shape, dt=f32):
            return es.enter_context(nc.sbuf_tensor(name, shape, dt))

        def sem(name):
            return es.enter_context(nc.semaphore(name))

        def ring(name, shape, dt=f32):
            return [sb(f"{name}{i}", shape, dt) for i in range(2)]

        ident = sb("ident", [P, P])
        wT_hi = sb("wT_hi", [P, 4, C, D], f32r)
        wT_lo = sb("wT_lo", [P, 4, C, D], f32r)
        XP, WR, WK, WV = range(4)
        wT_xp = sb("wT_xp", [P, C, D])
        bias_col = sb("bias_col", [P, C])
        mu = sb("mu", [P, 2, C])
        one_minus_mu = sb("one_minus_mu", [P, 2, C])
        neg_half = sb("neg_half", [P, 2 * T])
        mask_u8 = sb("mask_u8", [P, B * K], u8)
        mask_bias = sb("mask_bias", [P, B, K])
        X = sb("X", [P, B * TB, D])
        xn = sb("xn", [P, T, D])
        bn1 = sb("bn1", [P, T, 6])
        mv = sb("mv", [P, 2 * T, 2])
        ve = sb("ve", [P, 2 * T])
        rstd = sb("rstd", [P, 2 * T])
        nm2 = sb("nm2", [P, T])
        xnT_hi = sb("xnT_hi", [P, C, N], f32r)
        xnT_lo = sb("xnT_lo", [P, C, N], f32r)
        y = ring("y", [K, 2, D])
        yT = sb("yT", [P, C, KP])
        xp = sb("xp", [P, C, N])
        yp = sb("yp", [P, C, KP])
        sc = sb("sc", [P, T, K])
        nmx = sb("nmx", [P, T])
        prob = sb("prob", [P, T, K])
        psums = sb("psums", [P, T])
        rinv = sb("rinv", [P, T])
        probT = sb("probT", [K, N])
        x1_both = sb("x1", [P, 2, T, D])
        x1 = [x1_both[:, i, :, :] for i in range(2)]
        w_rows = x1_both[:, :, :, :].rearrange("p i (m c) d -> p (i m) c d", c=C)
        bn2 = sb("bn2", [P, T, 6])
        xn2 = sb("xn2", [P, T, D])
        z = sb("z", [P, C, 2, L + 1])
        mur_z = sb("mur_z", [P, C, N])
        muk_z = sb("muk_z", [P, C, N])
        mixr = sb("mixr", [P, C, N])
        mixr_hi = sb("mixr_hi", [P, C, N], f32r)
        mixr_lo = sb("mixr_lo", [P, C, N], f32r)
        mixk = sb("mixk", [P, C, N])
        mixk_hi = sb("mixk_hi", [P, C, N], f32r)
        mixk_lo = sb("mixk_lo", [P, C, N], f32r)
        kact = sb("kact", [P, C, N])
        kact_hi = sb("kact_hi", [P, C, N], f32r)
        kact_lo = sb("kact_lo", [P, C, N], f32r)
        th = sb("th", [P, T, D])
        g = sb("g", [P, T, D])

        swap = [es.enter_context(nc.psum_tensor(f"swap{i}", [P, 2, 512], f32)) for i in range(2)]
        fixed = es.enter_context(nc.psum_tensor("fixed", [P, 2, 512], f32))
        key_bank = es.enter_context(nc.psum_tensor("key_bank", [P, 512], f32))
        score_bank = es.enter_context(nc.psum_tensor("score_bank", [P, 512], f32))

        def rows(bank2):
            return bank2[:, :, :].rearrange("p c (t d) -> p (c t) d", d=D)

        w_loaded, small_loaded = sem("w_loaded"), sem("small_loaded")
        x_loaded = [sem("x_loaded0"), sem("x_loaded1")]
        y_loaded = [sem("y_loaded0"), sem("y_loaded1")]
        stored = sem("stored")
        ident_ready, pool_const = sem("ident_ready"), sem("pool_const")
        wT_done, wT_hi_ready, wT_lo_ready = sem("wT_done"), sem("wT_hi_ready"), sem("wT_lo_ready")
        dve_const = sem("dve_const")
        xnT_done, yT_done = sem("xnT_done"), sem("yT_done")
        xp_done, yp_done = sem("xp_done"), sem("yp_done")
        score_done, probT_done, attn_done = sem("score_done"), sem("probT_done"), sem("attn_done")
        zT_done, k_done, r_done, kv_done = sem("zT_done"), sem("k_done"), sem("r_done"), sem("kv_done")
        xnT_hi_ready, yT_ready = sem("xnT_hi_ready"), sem("yT_ready")
        xp_ready, yp_ready = sem("xp_ready"), sem("yp_ready")
        krelu_ready, kact_ready, kact_hi_ready = sem("krelu_ready"), sem("kact_ready"), sem("kact_hi_ready")
        z_ready, muk_z_ready, mur_z_ready = sem("z_ready"), sem("muk_z_ready"), sem("mur_z_ready")
        mixr_hi_ready = sem("mixr_hi_ready")
        prob_ready, th_ready, probT_ready = sem("prob_ready"), sem("th_ready"), sem("probT_ready")
        x1_ready, bn2_ready, mv2_ready = sem("x1_ready"), sem("bn2_ready"), sem("mv2_ready")
        bn1_ready, mv1_ready, xn_ready = sem("bn1_ready"), sem("mv1_ready"), sem("xn_ready")
        sc_ready, nmx_ready, rinv_ready = sem("sc_ready"), sem("nmx_ready"), sem("rinv_ready")
        mixr_ready, mixr_lo_ready = sem("mixr_ready"), sem("mixr_lo_ready")
        mixk_ready, mixk_hi_ready = sem("mixk_ready"), sem("mixk_hi_ready")
        g_ready = sem("g_ready")
        xnT_lo_ready = sem("xnT_lo_ready")
        ve_ready, rstd_ready = sem("ve_ready"), sem("rstd_ready")
        nm2_ready, xn2_ready = sem("nm2_ready"), sem("xn2_ready")
        kact_lo_ready, mixk_lo_ready, res_ready = sem("kact_lo_ready"), sem("mixk_lo_ready"), sem("res_ready")

        def live(p):
            return not isinstance(p, int) or 0 <= p < PAIRS

        def some(p):
            return not isinstance(p, int) or p >= 0

        def steps(eng, step):
            for u in range(FIRST, LOOP[0]):
                step(u, u % 2)
            with eng.Fori(LOOP[0] // 2, LOOP[1] // 2) as i:
                for s in range(2):
                    step(2 * i + s, s)
            for u in range(LOOP[1], LAST + 1):
                step(u, u % 2)

        block = es.enter_context(nc.Block())

        @block.sync
        def _(sp):
            def load_x(p, par):
                if some(p - 2):
                    sp.wait_ge(x_loaded[par], 8 * (p - par))
                sp.dma_start(X[:, bass.ds(T * p, T), :], x_rows[:, bass.ds(T * p, T), :]).then_inc(x_loaded[par], 16)

            def load_y(p, par):
                if some(p - 2):
                    sp.wait_ge(attn_done, 2 * (p - 2) + 2)
                sp.dma_start(y[par][:, :, :], ctx_rows[:, bass.ds(2 * p, 2), :]).then_inc(y_loaded[par], 16)

            def step(u, s):
                if live(u + 2):
                    load_x(u + 2, s)
                if live(u + 1):
                    load_y(u + 1, 1 - s)
                if live(u - 2):
                    sp.wait_ge(res_ready, 2 * (u - 2) + 2)
                    sp.dma_start(out_rows[:, bass.ds(T * (u - 2), T), :], g[:, :, :]).then_inc(stored, 16)

            steps(sp, step)
            sp.wait_ge(stored, 16 * PAIRS)

        @block.gpsimd
        def _(pool):
            pool.memset(ident[:, :], 0.0).then_inc(ident_ready, 1)
            pool.memset(neg_half[:, :], -0.5).then_inc(pool_const, 1)
            pool.wait_ge(ident_ready, 1)
            pool.affine_select(out=ident[:, :], in_=ident[:, :], compare_op=ALU.not_equal, fill=1.0,
                               base=0, pattern=[[-1, P]], channel_multiplier=1).then_inc(ident_ready, 1)
            pool.memset(z[:, :, :, 0:1], 0.0).then_inc(pool_const, 1)
            pool.wait_ge(pool_const, 2)

            def step(u, s):
                p = u - 2
                if live(p):
                    pool.wait_ge(mixr_hi_ready, p + 1)
                    if some(p - 1):
                        pool.wait_ge(r_done, 2 * p)
                    pool.tensor_tensor(mixr_lo[:, :, :], mixr[:, :, :], mixr_hi[:, :, :].bitcast(f32),
                                       ALU.subtract).then_inc(mixr_lo_ready, 1)
                if live(u + 1) or live(u - 1):
                    if live(u + 1):
                        pool.wait_ge(mv1_ready, u + 2)
                    if live(u - 1):
                        pool.wait_ge(mv2_ready, u)
                    a, z_ = (0 if live(u - 1) else T), (2 * T if live(u + 1) else T)
                    if some(u - 1):
                        pool.wait_ge(xn_ready, u + 1 if live(u) else PAIRS)
                    pool.nop(nofuse=True)
                    pool.tensor_scalar(ve[:, a:z_], mv[:, a:z_, 1], EPS, None, ALU.add).then_inc(ve_ready, 1)
                    if live(u - 1):
                        pool.tensor_scalar(nm2[:, :], mv[:, 0:T, 0], -1.0, None, ALU.mult).then_inc(nm2_ready, 1)
                    pool.wait_ge(ve_ready, u + 2)
                    pool.tensor_tensor(rstd[:, a:z_], ve[:, a:z_], neg_half[:, a:z_], ALU.pow).then_inc(rstd_ready, 1)
                p = u - 1
                if live(p):
                    pool.wait_ge(nm2_ready, p + 1)
                    pool.wait_ge(rstd_ready, u + 2)
                    if some(p - 1):
                        pool.wait_ge(zT_done, 2 * p)
                    pool.nop(nofuse=True)
                    for t in range(T):
                        i = pool.tensor_scalar(xn2[:, t, :], x1[1 - s][:, t, :], nm2[:, t:t + 1],
                                               rstd[:, t:t + 1], ALU.add, ALU.mult)
                    i.then_inc(xn2_ready, 1)
                p = u - 1
                if live(p):
                    pool.wait_ge(mixk_hi_ready, p + 1)
                    if some(p - 1):
                        pool.wait_ge(k_done, C * p)
                    pool.tensor_tensor(mixk_lo[:, :, :], mixk[:, :, :], mixk_hi[:, :, :].bitcast(f32),
                                       ALU.subtract).then_inc(mixk_lo_ready, 1)
            steps(pool, step)

        @block.scalar
        def _(act):
            for m, w in enumerate((W, W_r, W_k, W_v)):
                act.dma_start(w_rows[:, m, :, :], w.rearrange("(c p) d -> p c d", p=P)).then_inc(w_loaded, 16)
            with nc.allow_non_contiguous_dma(reason="three vectors of one value a partition"):
                act.dma_start(bias_col[:, :], b.rearrange("(c p) -> p c", p=P)).then_inc(small_loaded, 16)
                for i, m in enumerate((mu_r, mu_k)):
                    act.dma_start(mu[:, i, :], m.rearrange("(c p) -> p c", p=P)).then_inc(small_loaded, 16)
            act.dma_start(mask_u8[:, :], mask.rearrange("b k -> (b k)").partition_broadcast(P)).then_inc(small_loaded, 16)
            act.wait_ge(small_loaded, 64)
            act.wait_ge(wT_done, 1)
            act.activation(wT_xp[:, :, :], swap[0][:, 0, :], ACT.Copy).then_inc(wT_hi_ready, 1)
            for m in range(4):
                act.wait_ge(wT_done, m + 1)
                bank = (swap[0], swap[1])[m // 2][:, m % 2, :]
                act.activation(wT_hi[:, m, :, :], bank, ACT.Copy,
                               scale=0.5 if m == WV else 1.0).then_inc(wT_hi_ready, 1)

            def step(u, s):
                p = u - 2
                if live(p):
                    act.wait_ge(mixr_ready, p + 1)
                    if some(p - 1):
                        act.wait_ge(r_done, 2 * p)
                    act.activation(mixr_hi[:, :, :], mixr[:, :, :], ACT.Copy).then_inc(mixr_hi_ready, 1)
                p = u
                if live(p):
                    if some(p - 1):
                        act.wait_ge(score_done, p)
                    for c in range(C):
                        act.wait_ge(xp_done, C * p + c + 1)
                        act.activation(xp[:, c, :], swap[s][:, c, :], ACT.Relu,
                                       bias=bias_col[:, c:c + 1]).then_inc(xp_ready, 1)
                    act.wait_ge(yp_done, p + 1)
                    for c in range(C):
                        act.activation(yp[:, c, :], key_bank[:, c * KP:(c + 1) * KP], ACT.Relu,
                                       bias=bias_col[:, c:c + 1]).then_inc(yp_ready, 1)
                p = u - 2
                if live(p):
                    if some(p - 1):
                        act.wait_ge(kact_lo_ready, p)
                    for c in range(C):
                        act.wait_ge(k_done, C * p + c + 1)
                        act.activation(kact[:, c, :], swap[1 - s][:, c, :], ACT.Relu).then_inc(krelu_ready, 1)
                    act.wait_ge(krelu_ready, C * p + C)
                    act.activation(kact[:, :, :], kact[:, :, :], ACT.Square).then_inc(kact_ready, 1)
                    act.wait_ge(kact_ready, p + 1)
                    if some(p - 1):
                        act.wait_ge(kv_done, 2 * p)
                    act.activation(kact_hi[:, :, :], kact[:, :, :], ACT.Copy).then_inc(kact_hi_ready, 1)
                p = u
                if live(p):
                    act.wait_ge(nmx_ready, p + 1)
                    if some(p - 1):
                        act.wait_ge(probT_done, p)
                    for t in range(T):
                        i = act.activation(prob[:, t, :], sc[:, t, :], ACT.Exp, bias=nmx[:, t:t + 1],
                                           accum_out=psums[:, t:t + 1])
                    i.then_inc(prob_ready, 1)
                p = u - 2
                if live(p):
                    if some(p - 1):
                        act.wait_ge(g_ready, 2 * p)
                    for h in range(2):
                        act.wait_ge(r_done, 2 * p + h + 1)
                        act.activation(th[:, 2 * h:2 * h + 2, :], rows(fixed)[:, 2 * h:2 * h + 2, :], ACT.Tanh,
                                       scale=0.5).then_inc(th_ready, 1)
                for h in range(2):
                    p = u - 1
                    if live(p):
                        if h == 0 and some(p - 1):
                            act.wait_ge(mixk_ready, p)
                            act.wait_ge(mixr_ready, p)
                        act.wait_ge(zT_done, C * p + h + 1)
                        act.activation(z[:, h, :, 1:L + 1], swap[s][:, h, :].rearrange("p (b l) -> p b l", b=2),
                                       ACT.Copy).then_inc(z_ready, 1)
                        act.activation(muk_z[:, h, :], swap[s][:, h, :], ACT.Copy,
                                       scale=mu[:, 1, h:h + 1]).then_inc(muk_z_ready, 1)
                p = u
                if live(p):
                    act.wait_ge(probT_done, p + 1)
                    if some(p - 1):
                        act.wait_ge(attn_done, 2 * p)
                    act.activation(probT[:, :], key_bank[0:K, 0:N], ACT.Copy).then_inc(probT_ready, 1)
                p = u + 1
                if live(p):
                    if some(p - 1):
                        act.wait_ge(yp_done, p)
                    for c in range(C):
                        act.wait_ge(xnT_done, C * p + c + 1)
                        act.activation(xnT_hi[:, c, :], fixed[:, c, :], ACT.Copy).then_inc(xnT_hi_ready, 1)
                    act.wait_ge(yT_done, p + 1)
                    act.activation(yT[:, :, :], score_bank[:, 0:C * KP].rearrange("p (c k) -> p c k", c=C),
                                   ACT.Copy).then_inc(yT_ready, 1)
                p = u - 1
                if live(p):
                    act.wait_ge(mixk_ready, p + 1)
                    if some(p - 1):
                        act.wait_ge(k_done, C * p)
                    act.activation(mixk_hi[:, :, :], mixk[:, :, :], ACT.Copy).then_inc(mixk_hi_ready, 1)
                p = u - 1
                if live(p):
                    if some(p - 1):
                        act.wait_ge(mixr_ready, p)
                    act.wait_ge(z_ready, C * p + C)
                    for c in range(C):
                        act.activation(mur_z[:, c, :].rearrange("p (b l) -> p b l", b=2), z[:, c, :, 1:L + 1],
                                       ACT.Copy, scale=mu[:, 0, c:c + 1]).then_inc(mur_z_ready, 1)

            steps(act, step)

        @block.vector
        def _(dve):
            dve.wait_ge(small_loaded, 64)
            dve.tensor_scalar(one_minus_mu[:, :, :], mu[:, :, :], -1.0, 1.0, ALU.mult, ALU.add).then_inc(dve_const, 1)
            dve.tensor_scalar(mask_bias[:, :, :], mask_u8[:, :].rearrange("p (b k) -> p b k", k=K), -3e38, 3e38,
                              ALU.mult, ALU.mult).then_inc(dve_const, 1)
            for m in range(4):
                dve.wait_ge(wT_hi_ready, m + 2)
                bank = (swap[0], swap[1])[m // 2][:, m % 2, :].rearrange("p (c d) -> p c d", c=C)
                dve.scalar_tensor_tensor(wT_lo[:, m, :, :], bank, 0.5 if m == WV else 1.0,
                                         wT_hi[:, m, :, :].bitcast(f32), ALU.mult, ALU.subtract).then_inc(wT_lo_ready, 1)
            dve.wait_ge(dve_const, 2)
            dve.wait_ge(pool_const, 2)

            def step(u, s):
                p = u - 1
                if live(p):
                    dve.wait_ge(rinv_ready, p + 1)
                    if some(p - 2):
                        dve.wait_ge(res_ready, 2 * (p - 1))
                    for t in range(T):
                        if t % TB == 0:
                            dve.wait_ge(attn_done, 2 * p + t // TB + 1)
                        dve.scalar_tensor_tensor(x1[1 - s][:, t, :], rows(swap[1 - s])[:, t, :], rinv[:, t:t + 1],
                                                 X[:, T * p + t, :], ALU.mult, ALU.add).then_inc(x1_ready, 1)
                    for t in range(T):
                        dve.wait_ge(x1_ready, T * p + t + 1)
                        dve.bn_stats(bn2[:, t, :], x1[1 - s][:, t, :]).then_inc(bn2_ready, 1)
                    if some(p - 1):
                        dve.wait_ge(rstd_ready, u + 1)
                    dve.wait_ge(bn2_ready, T * p + T)
                    dve.nop(nofuse=True)
                    for t in range(T):
                        i = dve.bn_aggr(mv[:, t, :], bn2[:, t, :])
                    i.then_inc(mv2_ready, 1)
                p = u + 2
                if live(p):
                    dve.wait_ge(x_loaded[s], 8 * (p - s) + 16)
                    if some(p - 1):
                        dve.wait_ge(mv1_ready, p)
                    for t in range(T):
                        dve.bn_stats(bn1[:, t, :], X[:, T * p + t, :]).then_inc(bn1_ready, 1)
                p = u
                if live(p):
                    dve.wait_ge(score_done, p + 1)
                    dve.tensor_tensor(sc[:, :, :].rearrange("p (b t) k -> p b t k", b=2),
                                      score_bank[:, 0:T * K].rearrange("p (b t k) -> p b t k", b=2, k=K),
                                      mask_bias[:, bass.ds(2 * p, 2), :].unsqueeze(2).to_broadcast([P, 2, TB, K]),
                                      ALU.add).then_inc(sc_ready, 1)
                    dve.wait_ge(sc_ready, p + 1)
                    dve.tensor_reduce(nmx[:, :], sc[:, :, :], AX.X, ALU.max, negate=True).then_inc(nmx_ready, 1)
                p = u - 2
                if live(p):
                    dve.wait_ge(kact_hi_ready, p + 1)
                    if some(p - 1):
                        dve.wait_ge(kv_done, 2 * p)
                    dve.tensor_tensor(kact_lo[:, :, :], kact[:, :, :], kact_hi[:, :, :].bitcast(f32),
                                       ALU.subtract).then_inc(kact_lo_ready, 1)
                p = u + 1
                if live(p):
                    dve.wait_ge(rstd_ready, u + 2)
                    if some(p - 1):
                        dve.wait_ge(xnT_done, C * p)
                    for t in range(T):
                        i = dve.tensor_scalar(xn[:, t, :], X[:, T * p + t, :], mv[:, T + t, 0:1], rstd[:, T + t:T + t + 1],
                                              ALU.subtract, ALU.mult)
                    i.then_inc(xn_ready, 1)
                p = u + 2
                if live(p):
                    if some(p - 1):
                        dve.wait_ge(rstd_ready, u + 2)
                    if some(p - 1):
                        dve.wait_ge(xn_ready, p)
                    dve.wait_ge(bn1_ready, T * p + T)
                    dve.nop(nofuse=True)
                    for t in range(T):
                        i = dve.bn_aggr(mv[:, T + t, :], bn1[:, t, :])
                    i.then_inc(mv1_ready, 1)
                p = u
                if live(p):
                    dve.wait_ge(prob_ready, p + 1)
                    dve.reciprocal(rinv[:, :], psums[:, :]).then_inc(rinv_ready, 1)
                p = u - 1
                if live(p):
                    if some(p - 1):
                        dve.wait_ge(mixk_lo_ready, p)
                    for c in range(C):
                        dve.wait_ge(muk_z_ready, C * p + c + 1)
                        i = dve.scalar_tensor_tensor(mixk[:, c, :].rearrange("p (b l) -> p b l", b=2),
                                                     z[:, c, :, 0:L], one_minus_mu[:, 1, c:c + 1],
                                                     muk_z[:, c, :].rearrange("p (b l) -> p b l", b=2),
                                                     ALU.mult, ALU.add)
                    i.then_inc(mixk_ready, 1)
                p = u + 1
                if live(p):
                    for c in range(C):
                        dve.wait_ge(xnT_hi_ready, C * p + c + 1)
                        dve.tensor_tensor(xnT_lo[:, c, :], fixed[:, c, :], xnT_hi[:, c, :].bitcast(f32),
                                          ALU.subtract).then_inc(xnT_lo_ready, 1)
                p = u - 2
                if live(p):
                    if some(p - 1):
                        dve.wait_ge(stored, 16 * p)
                    for h in range(2):
                        dve.wait_ge(th_ready, 2 * p + h + 1)
                        dve.wait_ge(kv_done, 2 * p + h + 1)
                        dve.scalar_tensor_tensor(g[:, 2 * h:2 * h + 2, :], th[:, 2 * h:2 * h + 2, :], 1.0,
                                                 rows(swap[1 - s])[:, 2 * h:2 * h + 2, :], ALU.add,
                                                 ALU.mult).then_inc(g_ready, 1)
                    for h in range(2):
                        dve.wait_ge(g_ready, 2 * p + h + 1)
                        dve.tensor_tensor(g[:, 2 * h:2 * h + 2, :], g[:, 2 * h:2 * h + 2, :],
                                          x1[s][:, 2 * h:2 * h + 2, :], ALU.add).then_inc(res_ready, 1)
                p = u - 1
                if live(p):
                    if some(p - 1):
                        dve.wait_ge(mixr_lo_ready, p)
                    dve.wait_ge(mur_z_ready, C * p + C)
                    for c in range(C):
                        i = dve.scalar_tensor_tensor(mixr[:, c, :].rearrange("p (b l) -> p b l", b=2),
                                                     z[:, c, :, 0:L], one_minus_mu[:, 0, c:c + 1],
                                                     mur_z[:, c, :].rearrange("p (b l) -> p b l", b=2),
                                                     ALU.mult, ALU.add)
                    i.then_inc(mixr_ready, 1)
            steps(dve, step)

        @block.tensor
        def _(pe):
            pe.wait_ge(ident_ready, 2)
            pe.wait_ge(w_loaded, 64)
            for m in range(4):
                for ci in range(C):
                    for co in range(C):
                        i = pe.transpose(swap[m // 2][:, m % 2, ci * D + co * P:ci * D + (co + 1) * P],
                                         w_rows[:, m, co, ci * P:(ci + 1) * P], ident[:, :])
                i.then_inc(wT_done, 1)

            def three(o, st_hi, st_lo, mv_hi, mv_lo):
                for c in range(C):
                    pe.matmul(o, st_hi(c), mv_hi(c), start=(c == 0), stop=False)
                    pe.matmul(o, st_hi(c), mv_lo(c), start=False, stop=False)
                    i = pe.matmul(o, st_lo(c), mv_hi(c), start=False, stop=(c == C - 1))
                return i

            def step(u, s):
                p = u
                if live(p):
                    if isinstance(p, int) and p == 0:
                        pe.wait_ge(wT_lo_ready, 4)
                    if some(p - 3):
                        pe.wait_ge(g_ready, 2 * (p - 3) + 2)
                    pe.wait_ge(xnT_lo_ready, C * p + C)
                    for e in range(C):
                        three(swap[s][:, e, :], lambda c: wT_hi[:, XP, c, e * P:(e + 1) * P],
                              lambda c: wT_lo[:, XP, c, e * P:(e + 1) * P],
                              lambda c: xnT_hi[:, c, :], lambda c: xnT_lo[:, c, :]).then_inc(xp_done, 1)
                    pe.wait_ge(yT_ready, p + 1)
                    for e in range(C):
                        for c in range(C):
                            i = pe.matmul(key_bank[:, e * KP:(e + 1) * KP], wT_xp[:, c, e * P:(e + 1) * P],
                                          yT[:, c, :], start=(c == 0), stop=(c == C - 1))
                    i.then_inc(yp_done, 1)
                p = u - 2
                if live(p):
                    pe.wait_ge(mixk_lo_ready, p + 1)
                    for e in range(C):
                        if live(u - 1):
                            pe.wait_ge(x1_ready, T * (u - 1) + TB * (e + 1))
                        three(swap[1 - s][:, e, :], lambda c: wT_hi[:, WK, c, e * P:(e + 1) * P],
                              lambda c: wT_lo[:, WK, c, e * P:(e + 1) * P],
                              lambda c: mixk_hi[:, c, :], lambda c: mixk_lo[:, c, :]).then_inc(k_done, 1)
                p = u
                if live(p):
                    pe.wait_ge(xp_ready, C * p + C)
                    pe.wait_ge(yp_ready, C * p + C)
                    for t in range(T):
                        bk = t // TB
                        for c in range(C):
                            i = pe.matmul(score_bank[:, t * K:(t + 1) * K], xp[:, c, t * P:(t + 1) * P],
                                          yp[:, c, bk * K:(bk + 1) * K], start=(c == 0), stop=(c == C - 1))
                    i.then_inc(score_done, 1)

                def r_tiles(h):
                    p = u - 2
                    if not live(p):
                        return
                    if h == 0:
                        pe.wait_ge(mixr_lo_ready, p + 1)
                        if not live(u):
                            pe.wait_ge(th_ready, 2 * (u - 3) + 2)
                    for t in (2 * h, 2 * h + 1):
                        i = three(rows(fixed)[:, t, :], lambda c: mixr_hi[:, c, t * P:(t + 1) * P],
                                  lambda c: mixr_lo[:, c, t * P:(t + 1) * P],
                                  lambda c: wT_hi[:, WR, c, :], lambda c: wT_lo[:, WR, c, :])
                    i.then_inc(r_done, 1)

                def kv_tiles(h):
                    p = u - 2
                    if not live(p):
                        return
                    if h == 0:
                        pe.wait_ge(kact_lo_ready, p + 1)
                    for t in (2 * h, 2 * h + 1):
                        i = three(rows(swap[1 - s])[:, t, :], lambda c: kact_hi[:, c, t * P:(t + 1) * P],
                                  lambda c: kact_lo[:, c, t * P:(t + 1) * P],
                                  lambda c: wT_hi[:, WV, c, :], lambda c: wT_lo[:, WV, c, :])
                    i.then_inc(kv_done, 1)

                r_tiles(0)
                r_tiles(1)
                p = u - 1
                if live(p):
                    pe.wait_ge(xn2_ready, p + 1)
                    if not live(u):
                        pe.wait_ge(g_ready, 2 * (u - 3) + 2)
                    for c in range(C):
                        for t in range(T):
                            i = pe.transpose(swap[s][:, c, t * P:(t + 1) * P], xn2[:, t, c * P:(c + 1) * P],
                                             ident[:, :])
                        i.then_inc(zT_done, 1)
                p = u
                if live(p):
                    pe.wait_ge(prob_ready, p + 1)
                    for t in range(T):
                        i = pe.transpose(key_bank[0:K, t * P:(t + 1) * P], prob[:, t, :], ident[:, :])
                    i.then_inc(probT_done, 1)
                kv_tiles(0)
                p = u + 1
                if live(p):
                    pe.wait_ge(xn_ready, p + 1)
                    if some(u - 2):
                        pe.wait_ge(th_ready, 2 * (u - 2) + 2)
                    for c in range(C):
                        for t in range(T):
                            i = pe.transpose(fixed[:, c, t * P:(t + 1) * P], xn[:, t, c * P:(c + 1) * P], ident[:, :])
                        i.then_inc(xnT_done, 1)
                    pe.wait_ge(y_loaded[1 - s], 8 * (p - (1 - s)) + 16)
                    if some(p - 1):
                        pe.wait_ge(sc_ready, p)
                    for c in range(C):
                        for bk in range(2):
                            i = pe.transpose(score_bank[:, c * KP + bk * K:c * KP + (bk + 1) * K],
                                             y[1 - s][:, bk, c * P:(c + 1) * P], ident[0:K, 0:K])
                    i.then_inc(yT_done, 1)
                kv_tiles(1)
                p = u
                if live(p):
                    pe.wait_ge(probT_ready, p + 1)
                    if some(p - 1):
                        pe.wait_ge(muk_z_ready, C * p)
                    for t in range(T):
                        i = pe.matmul(rows(swap[s])[:, t, :], probT[:, t * P:(t + 1) * P],
                                      y[s][:, t // TB, :], start=True, stop=True)
                        if t % TB == TB - 1:
                            i.then_inc(attn_done, 1)

            steps(pe, step)


_INS = ['x', 'ctx_1024', 'mask_BxS2_bf0', 'L0_xattn_W', 'L0_xattn_b', 'L0_ffn_W_r', 'L0_ffn_W_k', 'L0_ffn_W_v',
        'L0_ffn_mu_r', 'L0_ffn_mu_k']


def kernel(**inputs):
    import numpy as _np
    import concourse.bacc as _bacc
    from concourse import mybir as _mybir
    from concourse.bass_utils import run_bass_kernel_spmd as _run

    nc = _bacc.Bacc("TRN2", target_bir_lowering=False, num_devices=1)
    arrays, args = {}, []
    for name in _INS:
        a = _np.ascontiguousarray(inputs[name])
        arrays[f"in_{name}_dram"] = a
        args.append(nc.dram_tensor(f"in_{name}_dram", a.shape, _mybir.dt.from_np(a.dtype), kind="ExternalInput").ap())
    shape = tuple(inputs["x"].shape)
    args.append(nc.dram_tensor("out_0_dram", shape, _mybir.dt.float32, kind="ExternalOutput").ap())
    xattn_rwkv_ffn_kernel(nc, *args)
    r = _run(nc, [arrays], core_ids=[0])
    return r.results[0]["out_0_dram"]
```

```python
import concourse.bass as bass
from concourse import mybir
from contextlib import ExitStack


def xattn_rwkv_ffn_kernel(nc, x, ctx, mask, W, b, W_r, W_k, W_v, mu_r, mu_k, out):
    f32, f32r, u8 = mybir.dt.float32, mybir.dt.float32r, mybir.dt.uint8
    ALU, ACT, AX = mybir.AluOpType, mybir.ActivationFunctionType, mybir.AxisListType

    B, L, D = x.shape
    K = ctx.shape[1]
    P = 128
    PAIRS = B // 2
    T = 2 * L // P
    TB = L // P
    N = 2 * L
    C = D // P
    KP = 2 * K
    EPS = 1e-5
    LOOP = (4, PAIRS - 2)
    SPLIT = 2

    x_rows = x.rearrange("b (t p) d -> p (b t) d", p=P)
    out_rows = out.rearrange("b (t p) d -> p (b t) d", p=P)
    ctx_rows = ctx.rearrange("b k d -> k b d")

    es = ExitStack()
    with es:
        def sb(name, shape, dt=f32):
            return es.enter_context(nc.sbuf_tensor(name, shape, dt))

        def sem(name):
            return es.enter_context(nc.semaphore(name))

        def ring(name, shape, dt=f32):
            return [sb(f"{name}{i}", shape, dt) for i in range(2)]

        ident = sb("ident", [P, P])
        wT_hi = sb("wT_hi", [P, 4, C, D], f32r)
        wT_lo = sb("wT_lo", [P, 4, C, D], f32r)
        XP, WR, WK, WV = range(4)
        wT_xp = sb("wT_xp", [P, C, D])
        bias_col = sb("bias_col", [P, C])
        mu = sb("mu", [P, 2, C])
        neg_half = sb("neg_half", [P, T])
        mask_u8 = sb("mask_u8", [P, B * K], u8)
        mask_bias = sb("mask_bias", [P, B, K])
        X = sb("X", [P, B * TB, D])
        xn = sb("xn", [P, T, D])
        bn1 = sb("bn1", [P, T, 6])
        mv1, mv2 = sb("mv1", [P, T, 2]), sb("mv2", [P, T, 2])
        ve1, ve2 = sb("ve1", [P, T]), sb("ve2", [P, T])
        rstd1, rstd2 = sb("rstd1", [P, T]), sb("rstd2", [P, T])
        nm2 = sb("nm2", [P, T])
        xnT_hi = sb("xnT_hi", [P, C, N], f32r)
        xnT_lo = sb("xnT_lo", [P, C, N], f32r)
        y = ring("y", [K, 2, D])
        yT = sb("yT", [P, C, KP])
        xp = sb("xp", [P, C, N])
        yp = sb("yp", [P, C, KP])
        sc = sb("sc", [P, T, K])
        nmx = sb("nmx", [P, T])
        prob = sb("prob", [P, T, K])
        psums = sb("psums", [P, T])
        rinv = sb("rinv", [P, T])
        probT = sb("probT", [K, N])
        probT_hi = sb("probT_hi", [K, N], f32r)
        probT_lo = sb("probT_lo", [K, N], f32r)
        y_hi = sb("y_hi", [K, 2, D], f32r)
        y_lo = sb("y_lo", [K, 2, D], f32r)
        x1_both = sb("x1", [P, 2, T, D])
        x1 = [x1_both[:, i, :, :] for i in range(2)]
        w_rows = x1_both[:, :, :, :].rearrange("p i (m c) d -> p (i m) c d", c=C)
        bn2 = sb("bn2", [P, T, 6])
        xn2 = sb("xn2", [P, T, D])
        z = sb("z", [P, C, 2, L + 1])
        dz = sb("dz", [P, C, N])
        mixr = sb("mixr", [P, C, N])
        mixr_hi = sb("mixr_hi", [P, C, N], f32r)
        mixr_lo = sb("mixr_lo", [P, C, N], f32r)
        mixk = sb("mixk", [P, C, N])
        mixk_hi = sb("mixk_hi", [P, C, N], f32r)
        mixk_lo = sb("mixk_lo", [P, C, N], f32r)
        kact = sb("kact", [P, C, N])
        kact_hi = sb("kact_hi", [P, C, N], f32r)
        kact_lo = sb("kact_lo", [P, C, N], f32r)
        th = sb("th", [P, T, D])
        g = sb("g", [P, T, D])

        swap = [es.enter_context(nc.psum_tensor(f"swap{i}", [P, 2, 512], f32)) for i in range(2)]
        fixed = es.enter_context(nc.psum_tensor("fixed", [P, 2, 512], f32))
        singles = es.enter_context(nc.psum_tensor("singles", [P, 2, 512], f32))
        key_bank, score_bank = singles[:, 0, :], singles[:, 1, :]

        def rows(bank2):
            return bank2[:, :, :].rearrange("p c (t d) -> p (c t) d", d=D)

        w_banks = [swap[0][:, 0, :], swap[1][:, 0, :], swap[1][:, 1, :], key_bank]

        mixk_last, kact_last = (xnT_hi, xnT_lo), (mixk_hi, mixk_lo)
        g_last = xn2
        g_before = rows(xp)
        x1_last = xn

        def banks(bank2):
            return [bank2[:, 0, :], bank2[:, 1, :]]

        w_loaded = [sem(f"w_loaded{m}") for m in range(4)]
        small_loaded = sem("small_loaded")
        x_loaded = [sem("x_loaded0"), sem("x_loaded1")]
        y_loaded = [sem("y_loaded0"), sem("y_loaded1")]
        stored = sem("stored")
        ident_ready, pool_const = sem("ident_ready"), sem("pool_const")
        wT_done, wT_hi_ready, wT_lo_ready = sem("wT_done"), sem("wT_hi_ready"), sem("wT_lo_ready")
        dve_const, table_loaded = sem("dve_const"), sem("table_loaded")
        xnT_done, yT_done = sem("xnT_done"), sem("yT_done")
        xp_done, yp_done = sem("xp_done"), sem("yp_done")
        score_done, probT_done, attn_done = sem("score_done"), sem("probT_done"), sem("attn_done")
        zT_done, k_done = sem("zT_done"), sem("k_done")
        r_done, kv_done = sem("r_done"), sem("kv_done")
        xnT_hi_ready, yT_ready = sem("xnT_hi_ready"), sem("yT_ready")
        xp_ready, yp_ready = sem("xp_ready"), sem("yp_ready")
        prob_ready, probT_ready = sem("prob_ready"), sem("probT_ready")
        y_hi_ready, probT_hi_ready = sem("y_hi_ready"), sem("probT_hi_ready")
        z_ready, mixr_hi_ready, mixk_hi_ready = sem("z_ready"), sem("mixr_hi_ready"), sem("mixk_hi_ready")
        krelu_ready, kact_ready, kact_hi_ready = sem("krelu_ready"), sem("kact_ready"), sem("kact_hi_ready")
        th_ready = sem("th_ready")
        bn1_ready, mv1_ready, xn_ready = sem("bn1_ready"), sem("mv1_ready"), sem("xn_ready")
        xnT_lo_ready = sem("xnT_lo_ready")
        sc_ready, nmx_ready, rinv_ready = sem("sc_ready"), sem("nmx_ready"), sem("rinv_ready")
        x1_ready, bn2_ready, mv2_ready = sem("x1_ready"), sem("bn2_ready"), sem("mv2_ready")
        mixr_ready, mixk_ready = sem("mixr_ready"), sem("mixk_ready")
        kact_lo_ready = sem("kact_lo_ready")
        g_ready, res_ready = sem("g_ready"), sem("res_ready")
        ve1_ready, rstd1_ready = sem("ve1_ready"), sem("rstd1_ready")
        ve2_ready, nm2_ready, rstd2_ready = sem("ve2_ready"), sem("nm2_ready"), sem("rstd2_ready")
        y_lo_ready, probT_lo_ready = sem("y_lo_ready"), sem("probT_lo_ready")
        xn2_ready, dz_ready = sem("xn2_ready"), sem("dz_ready")
        mixr_lo_ready, mixk_lo_ready = sem("mixr_lo_ready"), sem("mixk_lo_ready")

        def some(p):
            return not isinstance(p, int) or p >= 0

        def at(p, n):
            return isinstance(p, int) and p == n

        def loop(eng, step):
            for u in range(3, LOOP[0]):
                step(u, u % 2)
            with eng.Fori(LOOP[0] // 2, LOOP[1] // 2) as i:
                for s in range(2):
                    step(2 * i + s, s)
            for u in range(LOOP[1], PAIRS - 1):
                step(u, u % 2)

        def count(tiles):
            return tiles.stop - tiles.start

        block = es.enter_context(nc.Block())

        @block.sync
        def _(sp):
            def load_x(p, par):
                if some(p - 2):
                    sp.wait_ge(x_loaded[par], 8 * (p - par))
                sp.dma_start(X[:, bass.ds(T * p, T), :], x_rows[:, bass.ds(T * p, T), :]).then_inc(x_loaded[par], 16)

            def load_y(p, par):
                if some(p - 2):
                    sp.wait_ge(attn_done, 2 * (p - 2) + 2)
                sp.dma_start(y[par][:, :, :], ctx_rows[:, bass.ds(2 * p, 2), :]).then_inc(y_loaded[par], 16)

            def store(p, g=g):
                sp.wait_ge(res_ready, 2 * p + 2)
                sp.dma_start(out_rows[:, bass.ds(T * p, T), :], g[:, :, :]).then_inc(stored, 16)

            load_x(0, 0)
            load_x(1, 1)
            load_y(0, 0)
            with nc.allow_non_contiguous_dma(reason="three vectors of one value a partition"):
                sp.dma_start(bias_col[:, :], b.rearrange("(c p) -> p c", p=P)).then_inc(small_loaded, 16)
                for i, m in enumerate((mu_r, mu_k)):
                    sp.dma_start(mu[:, i, :], m.rearrange("(c p) -> p c", p=P)).then_inc(small_loaded, 16)
            load_x(2, 0)
            load_y(1, 1)
            load_x(3, 1)
            load_y(2, 0)

            def step(u, s):
                if not (at(u, PAIRS - 2)):
                    load_x(u + 2, s)
                load_y(u + 1, 1 - s)
                store(u - 2)

            step(2, 0)
            loop(sp, step)
            store(PAIRS - 3)
            store(PAIRS - 2, g_before)
            for h in range(2):
                sp.wait_ge(res_ready, 2 * (PAIRS - 1) + h + 1)
                sp.dma_start(out_rows[:, T * (PAIRS - 1) + 2 * h:T * (PAIRS - 1) + 2 * h + 2, :],
                             g_last[:, 2 * h:2 * h + 2, :]).then_inc(stored, 16)
            sp.wait_ge(stored, 16 * (PAIRS + 1))

        @block.gpsimd
        def _(pool):
            pool.memset(ident[:, :], 0.0).then_inc(ident_ready, 1)
            pool.memset(neg_half[:, :], -0.5).then_inc(pool_const, 1)
            pool.wait_ge(ident_ready, 1)
            pool.affine_select(out=ident[:, :], in_=ident[:, :], compare_op=ALU.not_equal, fill=1.0,
                               base=0, pattern=[[-1, P]], channel_multiplier=1).then_inc(ident_ready, 1)
            pool.memset(z[:, :, :, 0:1], 0.0).then_inc(pool_const, 1)
            pool.wait_ge(pool_const, 2)

            def mixr_low(p):
                pool.wait_ge(mixr_hi_ready, p + 1)
                if some(p - 1):
                    pool.wait_ge(r_done, 2 * p)
                pool.tensor_tensor(mixr_lo[:, :, :], mixr[:, :, :], mixr_hi[:, :, :].bitcast(f32),
                                   ALU.subtract).then_inc(mixr_lo_ready, 1)

            def mixk_low(p):
                if some(p - 1):
                    pool.wait_ge(k_done, C * p)
                for c in range(C):
                    pool.wait_ge(mixk_hi_ready, C * p + c + 1)
                    pool.tensor_tensor(mixk_lo[:, c, :], mixk[:, c, :], mixk_hi[:, c, :].bitcast(f32),
                                       ALU.subtract).then_inc(mixk_lo_ready, 1)

            def inv_std1(p):
                pool.wait_ge(mv1_ready, p + 1)
                if some(p - 1):
                    pool.wait_ge(xn_ready, p)
                pool.nop(nofuse=True)
                pool.tensor_scalar(ve1[:, :], mv1[:, :, 1], EPS, None, ALU.add).then_inc(ve1_ready, 1)
                pool.wait_ge(ve1_ready, p + 1)
                pool.tensor_tensor(rstd1[:, :], ve1[:, :], neg_half[:, :], ALU.pow).then_inc(rstd1_ready, 1)

            def inv_std2(p):
                pool.wait_ge(mv2_ready, p + 1)
                pool.nop(nofuse=True)
                pool.tensor_scalar(ve2[:, :], mv2[:, :, 1], EPS, None, ALU.add).then_inc(ve2_ready, 1)
                pool.tensor_scalar(nm2[:, :], mv2[:, :, 0], -1.0, None, ALU.mult).then_inc(nm2_ready, 1)
                pool.wait_ge(ve2_ready, p + 1)
                pool.tensor_tensor(rstd2[:, :], ve2[:, :], neg_half[:, :], ALU.pow).then_inc(rstd2_ready, 1)

            def norm2(p, x1):
                pool.wait_ge(nm2_ready, p + 1)
                pool.wait_ge(rstd2_ready, p + 1)
                if some(p - 1):
                    pool.wait_ge(zT_done, C * p)
                pool.nop(nofuse=True)
                for t in range(T):
                    i = pool.tensor_scalar(xn2[:, t, :], x1[:, t, :], nm2[:, t:t + 1],
                                           rstd2[:, t:t + 1], ALU.add, ALU.mult)
                i.then_inc(xn2_ready, 1)

            def y_low(p, par):
                pool.wait_ge(y_hi_ready, p - SPLIT + 1)
                pool.tensor_tensor(y_lo[:, :, :], y[par][:, :, :], y_hi[:, :, :].bitcast(f32),
                                   ALU.subtract).then_inc(y_lo_ready, 1)

            def probT_low(p):
                pool.wait_ge(probT_hi_ready, p - SPLIT + 1)
                for bk in range(2):
                    q = slice(bk * L, (bk + 1) * L)
                    pool.tensor_tensor(probT_lo[:, q], probT[:, q], probT_hi[:, q].bitcast(f32),
                                       ALU.subtract).then_inc(probT_lo_ready, 1)

            def difference(p, c):
                pool.wait_ge(z_ready, C * p + c + 1)
                pool.wait_ge(mixr_ready, p)
                pool.tensor_tensor(dz[:, c, :].rearrange("p (b l) -> p b l", b=2), z[:, c, :, 1:L + 1],
                                   z[:, c, :, 0:L], ALU.subtract).then_inc(dz_ready, 1)

            inv_std1(0)
            inv_std1(1)
            inv_std1(2)
            inv_std1(3)
            inv_std2(0)
            norm2(0, x1[0])
            y_low(2, 0)
            mixr_low(0)
            inv_std2(1)
            norm2(1, x1[1])
            probT_low(2)
            difference(1, 0)
            difference(1, 1)
            mixk_low(1)

            def step(u, s):
                y_low(u, s)
                mixr_low(u - 2)
                inv_std2(u - 1)
                norm2(u - 1, x1[1 - s])
                inv_std1(u + 1)
                difference(u - 1, 0)
                probT_low(u)
                difference(u - 1, 1)
                mixk_low(u - 1)

            loop(pool, step)
            mixr_low(PAIRS - 3)
            inv_std2(PAIRS - 2)
            norm2(PAIRS - 2, x1[0])
            mixk_low(PAIRS - 2)
            inv_std2(PAIRS - 1)

        @block.scalar
        def _(act):
            for m, w in enumerate((W, W_r, W_k, W_v)):
                act.dma_start(w_rows[:, m, :, :], w.rearrange("(c p) d -> p c d", p=P)).then_inc(w_loaded[m], 16)
            act.dma_start(mask_u8[:, :], mask.rearrange("b k -> (b k)").partition_broadcast(P)).then_inc(small_loaded, 16)
            act.wait_ge(pool_const, 1)
            act.activation(sc[:, 0, 0:T], neg_half[:, :], ACT.Copy).then_inc(table_loaded, 1)

            def weight_high(m):
                act.wait_ge(wT_done, m + 1)
                if m == XP:
                    act.activation(wT_xp[:, :, :], w_banks[XP], ACT.Copy).then_inc(wT_hi_ready, 1)
                act.activation(wT_hi[:, m, :, :], w_banks[m], ACT.Copy,
                               scale=0.5 if m == WV else 1.0).then_inc(wT_hi_ready, 1)

            def xn_high(p):
                if some(p - 1):
                    act.wait_ge(xp_done, C * p)
                for c in range(C):
                    act.wait_ge(xnT_done, C * p + c + 1)
                    act.activation(xnT_hi[:, c, :], fixed[:, c, :], ACT.Copy).then_inc(xnT_hi_ready, 1)

            def copy_yT(p):
                if some(p - 1):
                    act.wait_ge(yp_done, p)
                act.wait_ge(yT_done, p + 1)
                act.activation(yT[:, :, :], score_bank[:, 0:C * KP].rearrange("p (c k) -> p c k", c=C),
                               ACT.Copy).then_inc(yT_ready, 1)

            def relu_xp(p, par):
                if some(p - 1):
                    act.wait_ge(score_done, p)
                for c in range(C):
                    act.wait_ge(xp_done, C * p + c + 1)
                    act.activation(xp[:, c, :], swap[par][:, c, :], ACT.Relu,
                                   bias=bias_col[:, c:c + 1]).then_inc(xp_ready, 1)

            def relu_yp(p):
                act.wait_ge(yp_done, p + 1)
                for c in range(C):
                    act.activation(yp[:, c, :], key_bank[:, c * KP:(c + 1) * KP], ACT.Relu,
                                   bias=bias_col[:, c:c + 1]).then_inc(yp_ready, 1)

            def exponentials(p):
                act.wait_ge(nmx_ready, p + 1)
                if some(p - 1):
                    act.wait_ge(probT_done, p)
                for t in range(T):
                    i = act.activation(prob[:, t, :], sc[:, t, :], ACT.Exp, bias=nmx[:, t:t + 1],
                                       accum_out=psums[:, t:t + 1])
                i.then_inc(prob_ready, 1)

            def copy_probT(p, whole=False):
                act.wait_ge(probT_done, p + 1)
                if some(p - 1):
                    act.wait_ge(attn_done, 2 * p)
                act.activation(probT[:, :], key_bank[0:K, 0:N], ACT.Copy).then_inc(probT_ready, 1)
                if whole:
                    return
                act.activation(probT_hi[:, :], key_bank[0:K, 0:N], ACT.Copy).then_inc(probT_hi_ready, 1)

            def y_high(p, par):
                act.wait_ge(y_loaded[par], 8 * (p - par) + 16)
                if some(p - SPLIT - 1):
                    act.wait_ge(attn_done, 2 * p)
                act.activation(y_hi[:, :, :], y[par][:, :, :], ACT.Copy).then_inc(y_hi_ready, 1)

            def copy_z(p, bank2):
                if some(p - 1):
                    act.wait_ge(mixk_ready, C * p)
                    act.wait_ge(mixr_ready, p)
                for c in range(C):
                    act.wait_ge(zT_done, C * p + c + 1)
                    act.activation(z[:, c, :, 1:L + 1], bank2[:, c, :].rearrange("p (b l) -> p b l", b=2),
                                   ACT.Copy).then_inc(z_ready, 1)

            def mixk_high(p, hi, tiles=range(C)):
                if at(p, PAIRS - 1):
                    act.wait_ge(xp_done, C * PAIRS)
                elif some(p - 1):
                    act.wait_ge(k_done, C * p)
                for c in tiles:
                    act.wait_ge(mixk_ready, C * p + c + 1)
                    act.activation(hi[:, c, :], mixk[:, c, :], ACT.Copy).then_inc(mixk_hi_ready, 1)

            def mixr_high(p):
                act.wait_ge(mixr_ready, p + 1)
                if some(p - 1):
                    act.wait_ge(r_done, 2 * p)
                act.activation(mixr_hi[:, :, :], mixr[:, :, :], ACT.Copy).then_inc(mixr_hi_ready, 1)

            def relu_k(p, banks, tiles=range(C)):
                if some(p - 1):
                    act.wait_ge(kact_lo_ready, C * p)
                for c in tiles:
                    act.wait_ge(k_done, C * p + c + 1)
                    act.activation(kact[:, c, :], banks[c], ACT.Relu).then_inc(krelu_ready, 1)

            def square_k(p, hi, c=slice(0, C), n=C):
                act.wait_ge(krelu_ready, C * p + n)
                act.activation(kact[:, c, :], kact[:, c, :], ACT.Square).then_inc(kact_ready, count(c))
                act.wait_ge(kact_ready, C * p + n)
                if at(p, PAIRS - 1):
                    act.wait_ge(k_done, C * p)
                elif some(p - 1):
                    act.wait_ge(kv_done, 2 * p)
                act.activation(hi[:, c, :], kact[:, c, :], ACT.Copy).then_inc(kact_hi_ready, count(c))

            def tanh_r(p, bank2):
                if some(p - 1):
                    act.wait_ge(g_ready, 2 * p)
                for h in range(2):
                    act.wait_ge(r_done, 2 * p + h + 1)
                    act.activation(th[:, 2 * h:2 * h + 2, :], rows(bank2)[:, 2 * h:2 * h + 2, :], ACT.Tanh,
                                   scale=0.5).then_inc(th_ready, 1)

            weight_high(XP)
            weight_high(WR)
            xn_high(0)
            copy_yT(0)
            weight_high(WK)
            weight_high(WV)
            act.wait_ge(small_loaded, 64)
            relu_xp(0, 0)
            relu_yp(0)
            xn_high(1)
            exponentials(0)
            copy_probT(0, whole=True)
            copy_yT(1)
            relu_xp(1, 1)
            relu_yp(1)
            xn_high(2)
            exponentials(1)
            copy_probT(1, whole=True)
            copy_z(0, fixed)
            copy_yT(2)
            relu_xp(2, 0)
            mixk_high(0, mixk_hi, (0,))
            relu_yp(2)
            mixk_high(0, mixk_hi, (1,))
            y_high(2, 0)
            mixr_high(0)
            exponentials(2)
            relu_k(0, banks(fixed))
            square_k(0, kact_hi)
            copy_probT(2)
            tanh_r(0, fixed)
            copy_z(1, swap[0])
            xn_high(3)
            copy_yT(3)
            mixk_high(1, mixk_hi)

            def step(u, s):
                y_high(u, s)
                mixr_high(u - 2)
                relu_xp(u, s)
                relu_yp(u)
                relu_k(u - 2, banks(swap[1 - s]))
                square_k(u - 2, kact_hi)
                exponentials(u)
                tanh_r(u - 2, fixed)
                copy_z(u - 1, swap[s])
                copy_probT(u)
                xn_high(u + 1)
                copy_yT(u + 1)
                mixk_high(u - 1, mixk_hi)

            loop(act, step)
            mixr_high(PAIRS - 3)
            relu_xp(PAIRS - 1, 1)
            relu_yp(PAIRS - 1)
            relu_k(PAIRS - 3, banks(swap[0]))
            square_k(PAIRS - 3, kact_hi)
            exponentials(PAIRS - 1)
            tanh_r(PAIRS - 3, fixed)
            copy_probT(PAIRS - 1, whole=True)
            copy_z(PAIRS - 2, swap[1])
            mixk_high(PAIRS - 2, mixk_hi)
            relu_k(PAIRS - 2, banks(fixed), (0,))
            mixr_high(PAIRS - 2)
            relu_k(PAIRS - 2, banks(fixed), (1,))
            square_k(PAIRS - 2, kact_hi, slice(0, 1), 1)
            copy_z(PAIRS - 1, singles)
            square_k(PAIRS - 2, kact_hi, slice(1, 2), 2)
            mixk_high(PAIRS - 1, mixk_last[0])
            tanh_r(PAIRS - 2, swap[1])
            mixr_high(PAIRS - 1)
            relu_k(PAIRS - 1, banks(swap[0]))
            for c in range(C):
                square_k(PAIRS - 1, kact_last[0], slice(c, c + 1), c + 1)
            tanh_r(PAIRS - 1, singles)

        @block.vector
        def _(dve):
            def weight_low(m):
                dve.wait_ge(wT_hi_ready, m + 2)
                dve.scalar_tensor_tensor(wT_lo[:, m, :, :], w_banks[m].rearrange("p (c d) -> p c d", c=C),
                                         0.5 if m == WV else 1.0, wT_hi[:, m, :, :].bitcast(f32),
                                         ALU.mult, ALU.subtract).then_inc(wT_lo_ready, 1)

            def stats1(p, par):
                dve.wait_ge(x_loaded[par], 8 * (p - par) + 16)
                if some(p - 1):
                    dve.wait_ge(mv1_ready, p)
                for t in range(T):
                    dve.bn_stats(bn1[:, t, :], X[:, T * p + t, :]).then_inc(bn1_ready, 1)

            def aggregate1(p):
                if some(p - 1):
                    dve.wait_ge(rstd1_ready, p)
                    dve.wait_ge(xn_ready, p)
                dve.wait_ge(bn1_ready, T * p + T)
                dve.nop(nofuse=True)
                for t in range(T):
                    i = dve.bn_aggr(mv1[:, t, :], bn1[:, t, :])
                i.then_inc(mv1_ready, 1)

            def norm1(p):
                dve.wait_ge(rstd1_ready, p + 1)
                if some(p - 1):
                    dve.wait_ge(xnT_done, C * p)
                for t in range(T):
                    i = dve.tensor_scalar(xn[:, t, :], X[:, T * p + t, :], mv1[:, t, 0:1], rstd1[:, t:t + 1],
                                          ALU.subtract, ALU.mult)
                i.then_inc(xn_ready, 1)

            def xn_low(p):
                for c in range(C):
                    dve.wait_ge(xnT_hi_ready, C * p + c + 1)
                    dve.tensor_tensor(xnT_lo[:, c, :], fixed[:, c, :], xnT_hi[:, c, :].bitcast(f32),
                                      ALU.subtract).then_inc(xnT_lo_ready, 1)

            def mask_scores(p):
                dve.wait_ge(score_done, p + 1)
                dve.tensor_tensor(sc[:, :, :].rearrange("p (b t) k -> p b t k", b=2),
                                  score_bank[:, 0:T * K].rearrange("p (b t k) -> p b t k", b=2, k=K),
                                  mask_bias[:, bass.ds(2 * p, 2), :].unsqueeze(2).to_broadcast([P, 2, TB, K]),
                                  ALU.add).then_inc(sc_ready, 1)
                dve.wait_ge(sc_ready, p + 1)
                dve.tensor_reduce(nmx[:, :], sc[:, :, :], AX.X, ALU.max, negate=True).then_inc(nmx_ready, 1)

            def reciprocal_sums(p):
                dve.wait_ge(prob_ready, p + 1)
                dve.reciprocal(rinv[:, :], psums[:, :]).then_inc(rinv_ready, 1)

            def residual1(p, bank2, x1):
                dve.wait_ge(rinv_ready, p + 1)
                if at(p, PAIRS - 1):
                    dve.wait_ge(xnT_done, C * PAIRS)
                elif some(p - 2):
                    dve.wait_ge(res_ready, 2 * (p - 1))
                for t in range(T):
                    if t % TB == 0:
                        dve.wait_ge(attn_done, 2 * p + t // TB + 1)
                    dve.scalar_tensor_tensor(x1[:, t, :], rows(bank2)[:, t, :], rinv[:, t:t + 1],
                                             X[:, T * p + t, :], ALU.mult, ALU.add).then_inc(x1_ready, 1)

            def stats2(p, x1):
                for t in range(T):
                    dve.wait_ge(x1_ready, T * p + t + 1)
                    dve.bn_stats(bn2[:, t, :], x1[:, t, :]).then_inc(bn2_ready, 1)
                if some(p - 1):
                    dve.wait_ge(rstd2_ready, p)
                dve.wait_ge(bn2_ready, T * p + T)
                dve.nop(nofuse=True)
                for t in range(T):
                    i = dve.bn_aggr(mv2[:, t, :], bn2[:, t, :])
                i.then_inc(mv2_ready, 1)

            def difference(p):
                for c in range(C):
                    dve.wait_ge(z_ready, C * p + c + 1)
                    dve.tensor_tensor(dz[:, c, :].rearrange("p (b l) -> p b l", b=2), z[:, c, :, 1:L + 1],
                                      z[:, c, :, 0:L], ALU.subtract).then_inc(dz_ready, 1)

            def mix(o, which, c):
                return dve.scalar_tensor_tensor(
                    o[:, c, :].rearrange("p (b l) -> p b l", b=2), dz[:, c, :].rearrange("p (b l) -> p b l", b=2),
                    mu[:, which, c:c + 1], z[:, c, :, 0:L], ALU.mult, ALU.add)

            def mix_k(p, tiles=range(C)):
                if some(p - 1):
                    dve.wait_ge(mixk_lo_ready, C * p)
                for c in tiles:
                    dve.wait_ge(dz_ready, C * p + c + 1)
                    mix(mixk, 1, c).then_inc(mixk_ready, 1)

            def mix_r(p):
                if some(p - 1):
                    dve.wait_ge(mixr_lo_ready, p)
                dve.wait_ge(dz_ready, C * p + C)
                for c in range(C):
                    i = mix(mixr, 0, c)
                i.then_inc(mixr_ready, 1)

            def mixk_low(p, hi_lo, tiles=range(C)):
                for c in tiles:
                    dve.wait_ge(mixk_hi_ready, C * p + c + 1)
                    dve.tensor_tensor(hi_lo[1][:, c, :], mixk[:, c, :], hi_lo[0][:, c, :].bitcast(f32),
                                      ALU.subtract).then_inc(mixk_lo_ready, 1)

            def kact_low(p, hi_lo, c=slice(0, C), n=C):
                dve.wait_ge(kact_hi_ready, C * p + n)
                if some(p - 1) and not at(p, PAIRS - 1):
                    dve.wait_ge(kv_done, 2 * p)
                dve.tensor_tensor(hi_lo[1][:, c, :], kact[:, c, :], hi_lo[0][:, c, :].bitcast(f32),
                                  ALU.subtract).then_inc(kact_lo_ready, count(c))

            def mixr_low(p):
                dve.wait_ge(mixr_hi_ready, p + 1)
                dve.wait_ge(r_done, 2 * p)
                dve.tensor_tensor(mixr_lo[:, :, :], mixr[:, :, :], mixr_hi[:, :, :].bitcast(f32),
                                  ALU.subtract).then_inc(mixr_lo_ready, 1)

            def norm2(p, x1):
                dve.wait_ge(rstd2_ready, p + 1)
                dve.wait_ge(zT_done, C * p)
                for t in range(T):
                    i = dve.tensor_scalar(xn2[:, t, :], x1[:, t, :], mv2[:, t, 0:1], rstd2[:, t:t + 1],
                                          ALU.subtract, ALU.mult)
                i.then_inc(xn2_ready, 1)

            def gate(p, bank2, h, g=g):
                if h == 0 and at(p, PAIRS - 1):
                    dve.wait_ge(zT_done, C * PAIRS)
                elif h == 0 and at(p, PAIRS - 2):
                    dve.wait_ge(score_done, PAIRS)
                elif h == 0 and some(p - 1):
                    dve.wait_ge(stored, 16 * p)
                dve.wait_ge(th_ready, 2 * p + h + 1)
                dve.wait_ge(kv_done, 2 * p + h + 1)
                dve.scalar_tensor_tensor(g[:, 2 * h:2 * h + 2, :], th[:, 2 * h:2 * h + 2, :], 1.0,
                                         rows(bank2)[:, 2 * h:2 * h + 2, :], ALU.add, ALU.mult).then_inc(g_ready, 1)

            def residual2(p, x1, h, g=g):
                dve.wait_ge(g_ready, 2 * p + h + 1)
                dve.tensor_tensor(g[:, 2 * h:2 * h + 2, :], g[:, 2 * h:2 * h + 2, :],
                                  x1[:, 2 * h:2 * h + 2, :], ALU.add).then_inc(res_ready, 1)

            stats1(0, 0)
            aggregate1(0)
            norm1(0)
            stats1(1, 1)
            aggregate1(1)
            weight_low(XP)
            xn_low(0)
            weight_low(WR)
            weight_low(WK)
            weight_low(WV)
            norm1(1)
            stats1(2, 0)
            aggregate1(2)
            dve.wait_ge(small_loaded, 64)
            dve.tensor_scalar(mask_bias[:, :, :], mask_u8[:, :].rearrange("p (b k) -> p b k", k=K), -3e38, 3e38,
                              ALU.mult, ALU.mult).then_inc(dve_const, 1)
            dve.wait_ge(dve_const, 1)
            dve.wait_ge(pool_const, 2)
            dve.wait_ge(table_loaded, 1)
            xn_low(1)
            mask_scores(0)
            norm1(2)
            reciprocal_sums(0)
            stats1(3, 1)
            aggregate1(3)
            residual1(0, swap[0], x1[0])
            stats2(0, x1[0])
            xn_low(2)
            mask_scores(1)
            reciprocal_sums(1)
            norm1(3)
            difference(0)
            mix_k(0)
            mixk_low(0, (mixk_hi, mixk_lo), (0,))
            mix_r(0)
            mixk_low(0, (mixk_hi, mixk_lo), (1,))
            mask_scores(2)
            residual1(1, swap[1], x1[1])
            stats2(1, x1[1])
            kact_low(0, (kact_hi, kact_lo))
            stats1(4, 0)
            reciprocal_sums(2)
            aggregate1(4)
            gate(0, swap[1], 0)
            xn_low(3)
            gate(0, swap[1], 1)
            mix_k(1)
            residual2(0, x1[0], 0)
            residual2(0, x1[0], 1)
            mix_r(1)

            def step(u, s):
                residual1(u - 1, swap[1 - s], x1[1 - s])
                stats2(u - 1, x1[1 - s])
                if not at(u, PAIRS - 2):
                    stats1(u + 2, s)
                mask_scores(u)
                kact_low(u - 2, (kact_hi, kact_lo))
                reciprocal_sums(u)
                norm1(u + 1)
                if not at(u, PAIRS - 2):
                    aggregate1(u + 2)
                mix_k(u - 1, (0,))
                gate(u - 2, swap[1 - s], 0)
                xn_low(u + 1)
                gate(u - 2, swap[1 - s], 1)
                mix_k(u - 1, (1,))
                residual2(u - 2, x1[s], 0)
                residual2(u - 2, x1[s], 1)
                mix_r(u - 1)

            loop(dve, step)
            residual1(PAIRS - 2, swap[0], x1[0])
            stats2(PAIRS - 2, x1[0])
            mask_scores(PAIRS - 1)
            kact_low(PAIRS - 3, (kact_hi, kact_lo))
            reciprocal_sums(PAIRS - 1)
            difference(PAIRS - 2)
            mix_k(PAIRS - 2)
            residual1(PAIRS - 1, singles, x1_last)
            stats2(PAIRS - 1, x1_last)
            mix_r(PAIRS - 2)
            norm2(PAIRS - 1, x1_last)
            mixr_low(PAIRS - 2)
            gate(PAIRS - 3, swap[0], 0)
            kact_low(PAIRS - 2, (kact_hi, kact_lo), slice(0, 1), 1)
            difference(PAIRS - 1)
            gate(PAIRS - 3, swap[0], 1)
            kact_low(PAIRS - 2, (kact_hi, kact_lo), slice(1, 2), 2)
            mix_k(PAIRS - 1)
            mixk_low(PAIRS - 1, mixk_last)
            mix_r(PAIRS - 1)
            for h in range(2):
                residual2(PAIRS - 3, x1[1], h)
            mixr_low(PAIRS - 1)
            for h in range(2):
                gate(PAIRS - 2, fixed, h, g_before)
            for c in range(C):
                kact_low(PAIRS - 1, kact_last, slice(c, c + 1), c + 1)
            for h in range(2):
                residual2(PAIRS - 2, x1[0], h, g_before)
            for h in range(2):
                gate(PAIRS - 1, swap[0], h, g_last)
                residual2(PAIRS - 1, x1_last, h, g_last)

        @block.tensor
        def _(pe):
            pe.wait_ge(ident_ready, 2)

            def three(o, st_hi, st_lo, mv_hi, mv_lo, tiles=C):
                for c in range(tiles):
                    pe.matmul(o, st_hi(c), mv_hi(c), start=(c == 0), stop=False)
                    pe.matmul(o, st_hi(c), mv_lo(c), start=False, stop=False)
                    i = pe.matmul(o, st_lo(c), mv_hi(c), start=False, stop=(c == tiles - 1))
                return i

            def transpose_weight(m):
                pe.wait_ge(w_loaded[m], 16)
                for ci in range(C):
                    for co in range(C):
                        i = pe.transpose(w_banks[m][:, ci * D + co * P:ci * D + (co + 1) * P],
                                         w_rows[:, m, co, ci * P:(ci + 1) * P], ident[:, :])
                i.then_inc(wT_done, 1)

            def transpose_xn(p):
                pe.wait_ge(xn_ready, p + 1)
                if some(p - 3):
                    pe.wait_ge(th_ready, 2 * (p - 3) + 2)
                elif some(p - 1):
                    pe.wait_ge(xnT_lo_ready, C * p)
                for c in range(C):
                    for t in range(T):
                        i = pe.transpose(fixed[:, c, t * P:(t + 1) * P], xn[:, t, c * P:(c + 1) * P], ident[:, :])
                    i.then_inc(xnT_done, 1)

            def transpose_y(p, par):
                pe.wait_ge(y_loaded[par], 8 * (p - par) + 16)
                if some(p - 1):
                    pe.wait_ge(sc_ready, p)
                for c in range(C):
                    for bk in range(2):
                        i = pe.transpose(score_bank[:, c * KP + bk * K:c * KP + (bk + 1) * K],
                                         y[par][:, bk, c * P:(c + 1) * P], ident[0:K, 0:K])
                i.then_inc(yT_done, 1)

            def project_x(p, par):
                if some(p - 3):
                    pe.wait_ge(g_ready, 2 * (p - 3) + 2)
                elif some(p - 2):
                    pe.wait_ge(x1_ready, T * (p - 1))
                elif some(p - 1):
                    pe.wait_ge(wT_lo_ready, 4)
                else:
                    pe.wait_ge(wT_lo_ready, 1)
                pe.wait_ge(xnT_lo_ready, C * p + C)
                for e in range(C):
                    three(swap[par][:, e, :], lambda c: wT_hi[:, XP, c, e * P:(e + 1) * P],
                          lambda c: wT_lo[:, XP, c, e * P:(e + 1) * P],
                          lambda c: xnT_hi[:, c, :], lambda c: xnT_lo[:, c, :]).then_inc(xp_done, 1)

            def project_y(p):
                if at(p, 0):
                    pe.wait_ge(wT_lo_ready, 4)
                pe.wait_ge(yT_ready, p + 1)
                for e in range(C):
                    for c in range(C):
                        i = pe.matmul(key_bank[:, e * KP:(e + 1) * KP], wT_xp[:, c, e * P:(e + 1) * P],
                                      yT[:, c, :], start=(c == 0), stop=(c == C - 1))
                i.then_inc(yp_done, 1)

            def scores(p):
                pe.wait_ge(xp_ready, C * p + C)
                pe.wait_ge(yp_ready, C * p + C)
                for t in range(T):
                    bk = t // TB
                    for c in range(C):
                        i = pe.matmul(score_bank[:, t * K:(t + 1) * K], xp[:, c, t * P:(t + 1) * P],
                                      yp[:, c, bk * K:(bk + 1) * K], start=(c == 0), stop=(c == C - 1))
                i.then_inc(score_done, 1)

            def transpose_prob(p):
                pe.wait_ge(prob_ready, p + 1)
                for t in range(T):
                    i = pe.transpose(key_bank[0:K, t * P:(t + 1) * P], prob[:, t, :], ident[:, :])
                i.then_inc(probT_done, 1)

            def attend_whole(p, bank2, par):
                pe.wait_ge(probT_ready, p + 1)
                for t in range(T):
                    i = pe.matmul(rows(bank2)[:, t, :], probT[:, t * P:(t + 1) * P], y[par][:, t // TB, :],
                                  start=True, stop=True)
                    if t % TB == TB - 1:
                        i.then_inc(attn_done, 1)

            def attend(p, bank2):
                pe.wait_ge(y_lo_ready, p - SPLIT + 1)
                for t in range(T):
                    if t % TB == 0:
                        pe.wait_ge(probT_lo_ready, 2 * (p - SPLIT) + t // TB + 1)
                    i = three(rows(bank2)[:, t, :], lambda c: probT_hi[:, t * P:(t + 1) * P],
                              lambda c: probT_lo[:, t * P:(t + 1) * P],
                              lambda c: y_hi[:, t // TB, :], lambda c: y_lo[:, t // TB, :], tiles=1)
                    if t % TB == TB - 1:
                        i.then_inc(attn_done, 1)

            def transpose_xn2(p, bank2):
                pe.wait_ge(xn2_ready, p + 1)
                for c in range(C):
                    for t in range(T):
                        i = pe.transpose(bank2[:, c, t * P:(t + 1) * P], xn2[:, t, c * P:(c + 1) * P], ident[:, :])
                    i.then_inc(zT_done, 1)

            def channel_k(p, hi_lo, banks, free):
                pe.wait_ge(mixk_lo_ready, C * p + C)
                for e in range(C):
                    pe.wait_ge(*free(e))
                    three(banks[e], lambda c: wT_hi[:, WK, c, e * P:(e + 1) * P],
                          lambda c: wT_lo[:, WK, c, e * P:(e + 1) * P],
                          lambda c: hi_lo[0][:, c, :], lambda c: hi_lo[1][:, c, :]).then_inc(k_done, 1)

            def channel_r(p, bank2, h):
                if h == 0:
                    pe.wait_ge(mixr_lo_ready, p + 1)
                for t in (2 * h, 2 * h + 1):
                    i = three(rows(bank2)[:, t, :], lambda c: mixr_hi[:, c, t * P:(t + 1) * P],
                              lambda c: mixr_lo[:, c, t * P:(t + 1) * P],
                              lambda c: wT_hi[:, WR, c, :], lambda c: wT_lo[:, WR, c, :])
                i.then_inc(r_done, 1)

            def channel_kv(p, hi_lo, bank2, h):
                if h == 0:
                    pe.wait_ge(kact_lo_ready, C * p + C)
                for t in (2 * h, 2 * h + 1):
                    i = three(rows(bank2)[:, t, :], lambda c: hi_lo[0][:, c, t * P:(t + 1) * P],
                              lambda c: hi_lo[1][:, c, t * P:(t + 1) * P],
                              lambda c: wT_hi[:, WV, c, :], lambda c: wT_lo[:, WV, c, :])
                i.then_inc(kv_done, 1)

            transpose_weight(XP)
            transpose_weight(WR)
            transpose_xn(0)
            transpose_y(0, 0)
            transpose_weight(WK)
            transpose_weight(WV)
            project_x(0, 0)
            project_y(0)
            transpose_xn(1)
            scores(0)
            project_x(1, 1)
            transpose_prob(0)
            transpose_y(1, 1)
            attend_whole(0, swap[0], 0)
            project_y(1)
            transpose_xn(2)
            scores(1)
            project_x(2, 0)
            transpose_prob(1)
            transpose_y(2, 0)
            transpose_xn2(0, fixed)
            attend_whole(1, swap[1], 1)
            project_y(2)
            scores(2)
            channel_k(0, (mixk_hi, mixk_lo), banks(fixed), lambda e: (z_ready, C))
            transpose_prob(2)
            pe.wait_ge(krelu_ready, C)
            channel_r(0, fixed, 0)
            channel_r(0, fixed, 1)
            transpose_y(3, 1)
            pe.wait_ge(x1_ready, 2 * T)
            channel_kv(0, (kact_hi, kact_lo), swap[1], 0)
            transpose_xn2(1, swap[0])
            transpose_xn(3)
            channel_kv(0, (kact_hi, kact_lo), swap[1], 1)
            pe.wait_ge(z_ready, C * 2)
            attend(2, swap[0])

            def step(u, s):
                project_x(u, s)
                project_y(u)
                channel_k(u - 2, (mixk_hi, mixk_lo), banks(swap[1 - s]), lambda e: (x1_ready, T * (u - 1) + TB * (e + 1)))
                scores(u)
                channel_r(u - 2, fixed, 0)
                channel_r(u - 2, fixed, 1)
                transpose_xn2(u - 1, swap[s])
                transpose_prob(u)
                channel_kv(u - 2, (kact_hi, kact_lo), swap[1 - s], 0)
                transpose_xn(u + 1)
                transpose_y(u + 1, 1 - s)
                channel_kv(u - 2, (kact_hi, kact_lo), swap[1 - s], 1)
                pe.wait_ge(z_ready, C * u)
                attend(u, swap[s])

            loop(pe, step)
            p = PAIRS - 1
            project_x(p, 1)
            project_y(p)
            channel_k(p - 2, (mixk_hi, mixk_lo), banks(swap[0]), lambda e: (x1_ready, T * (p - 1) + TB * (e + 1)))
            scores(p)
            channel_r(p - 2, fixed, 0)
            channel_r(p - 2, fixed, 1)
            transpose_prob(p)
            transpose_xn2(p - 1, swap[1])
            attend_whole(p, singles, 1)
            channel_kv(p - 2, (kact_hi, kact_lo), swap[0], 0)
            channel_kv(p - 2, (kact_hi, kact_lo), swap[0], 1)
            channel_k(p - 1, (mixk_hi, mixk_lo), banks(fixed), lambda e: (th_ready, 2 * (p - 2) + 2))
            pe.wait_ge(x1_ready, T * PAIRS)
            transpose_xn2(p, singles)
            pe.wait_ge(z_ready, C * p)
            channel_r(p - 1, swap[1], 0)
            channel_r(p - 1, swap[1], 1)
            channel_kv(p - 1, (kact_hi, kact_lo), fixed, 0)
            channel_kv(p - 1, (kact_hi, kact_lo), fixed, 1)
            channel_k(p, mixk_last, banks(swap[0]), lambda e: (g_ready, 2 * (p - 2) + 2))
            pe.wait_ge(z_ready, C * PAIRS)
            channel_r(p, singles, 0)
            channel_r(p, singles, 1)
            channel_kv(p, kact_last, swap[0], 0)
            channel_kv(p, kact_last, swap[0], 1)


_INS = ['x', 'ctx_1024', 'mask_BxS2_bf0', 'L0_xattn_W', 'L0_xattn_b', 'L0_ffn_W_r', 'L0_ffn_W_k', 'L0_ffn_W_v',
        'L0_ffn_mu_r', 'L0_ffn_mu_k']


def kernel(**inputs):
    import numpy as _np
    import concourse.bacc as _bacc
    from concourse import mybir as _mybir
    from concourse.bass_utils import run_bass_kernel_spmd as _run

    nc = _bacc.Bacc("TRN2", target_bir_lowering=False, num_devices=1)
    arrays, args = {}, []
    for name in _INS:
        a = _np.ascontiguousarray(inputs[name])
        arrays[f"in_{name}_dram"] = a
        args.append(nc.dram_tensor(f"in_{name}_dram", a.shape, _mybir.dt.from_np(a.dtype), kind="ExternalInput").ap())
    shape = tuple(inputs["x"].shape)
    args.append(nc.dram_tensor("out_0_dram", shape, _mybir.dt.float32, kind="ExternalOutput").ap())
    xattn_rwkv_ffn_kernel(nc, *args)
    r = _run(nc, [arrays], core_ids=[0])
    return r.results[0]["out_0_dram"]
```
